# Optimizing a Trainium2 kernel written in Bass

```python
import numpy as np
import jax
import jax.numpy as jnp

def _softmax(x, axis=-1):
    return jax.nn.softmax(x, axis=axis)

def _gelu(x):
    return jax.nn.gelu(x, approximate=True)

def _silu(x):
    return jax.nn.silu(x)

def _sigmoid(x):
    return jax.nn.sigmoid(x)

def _layernorm(x, axis=-1, eps=1e-05):
    m = jnp.mean(x, axis=axis, keepdims=True)
    v = jnp.var(x, axis=axis, keepdims=True)
    return (x - m) / jnp.sqrt(v + eps)

def _scatter_add(tgt, idx, src, axis=0):
    return tgt.at[idx].add(src)

def _segment_sum(src, seg, n):
    return jax.ops.segment_sum(src, seg, n)
kernel_name = 'mk_xattn_ffn_d2_seqx_r8_7c570b'

def setup_inputs(seed: int=0):
    np.random.seed(seed)
    _w = jnp.asarray

    def _rec_inputs():
        import jax
        import jax.numpy as jnp
        _rk = jax.random.key(seed)
        x = 7.22e-05 + 1 * jax.random.normal(jax.random.fold_in(_rk, 1), (4, 512, 128), jnp.float32)
        _lenS = 512 - jax.random.randint(jax.random.fold_in(_rk, 7), (4,), 0, max(1, 512 // 4) + 1, jnp.int32)
        _lenS2 = 77 - jax.random.randint(jax.random.fold_in(_rk, 8), (4,), 0, max(1, 77 // 4) + 1, jnp.int32)
        _ctx_1024P = jax.random.normal(jax.random.fold_in(_rk, 11), (4, 16, 128), jnp.float32)
        _ctx_1024c = jax.random.dirichlet(jax.random.fold_in(_rk, 511), 0.3 * jnp.ones((16,), jnp.float32), (4, 77))
        _ctx_1024t = jnp.einsum('bsk,bkd->bsd', _ctx_1024c, _ctx_1024P)
        _ctx_1024t = _ctx_1024t * jax.lax.rsqrt(jnp.mean(jnp.square(_ctx_1024t)) + 1e-12) * 0.953939
        ctx_1024 = 4.13588e-05 + 0.999923 * (_ctx_1024t + 0.3 * jax.random.normal(jax.random.fold_in(_rk, 611), (4, 77, 128), jnp.float32))
        _validS = jnp.arange(512)[None, :] < _lenS[:, None]
        _validS2 = jnp.arange(77)[None, :] < _lenS2[:, None]
        _causal = jnp.tril(jnp.ones((512, 512), dtype=bool))
        mask_Bx1x1xS2_bf1 = jnp.ones((4, 1, 1, 77), dtype=bool)
        return (x, ctx_1024, mask_Bx1x1xS2_bf1)
    x, ctx_1024, mask_Bx1x1xS2_bf1 = _rec_inputs()

    def _L0_xattn_setup():
        import jax, jax.numpy as jnp
        import numpy as np
        D_MODEL = 128
        NUM_HEADS = 16
        D_K = D_MODEL // NUM_HEADS
        key = jax.random.key(seed)
        ks = jax.random.split(key, 12)
        b, t1, t2 = (4, 256, 256)
        s = 1.0 / np.sqrt(D_MODEL)
        inp = {'q': jax.random.normal(ks[0], (b, t1, D_MODEL), jnp.float32), 'k': jax.random.normal(ks[1], (b, t2, D_MODEL), jnp.float32), 'v': jax.random.normal(ks[2], (b, t2, D_MODEL), jnp.float32), 'mask': jnp.ones((b, 1, 1, t2), dtype=bool), 'w_q': jax.random.normal(ks[3], (D_MODEL, D_MODEL), jnp.float32) * s, 'b_q': jax.random.normal(ks[4], (D_MODEL,), jnp.float32) * s, 'w_k': jax.random.normal(ks[5], (D_MODEL, D_MODEL), jnp.float32) * s, 'b_k': jax.random.normal(ks[6], (D_MODEL,), jnp.float32) * s, 'w_v': jax.random.normal(ks[7], (D_MODEL, D_MODEL), jnp.float32) * s, 'b_v': jax.random.normal(ks[8], (D_MODEL,), jnp.float32) * s, 'w_o': jax.random.normal(ks[9], (D_MODEL, D_MODEL), jnp.float32) * s, 'b_o': jax.random.normal(ks[10], (D_MODEL,), jnp.float32) * s}
        return inp
    _L0_xattn_all = _L0_xattn_setup()
    _L0_xattn_in = {k: v for k, v in _L0_xattn_all.items() if k in ('w_q', 'b_q', 'w_k', 'b_k', 'w_v', 'b_v', 'w_o', 'b_o')}
    del _L0_xattn_all

    def _L0_ffn_setup():
        import jax, jax.numpy as jnp
        import numpy as np
        DIM = 128
        DEPTH = 6
        HEADS = 16
        DIM_HEAD = 64
        WINDOW = 32
        INNER = HEADS * DIM_HEAD
        DIM_INNER = int(DIM * 4 * 2 / 3)
        QK_SCALE = 8.0

        def shift_tokens(t):
            a, s = jnp.split(t, 2, -1)
            s = jnp.pad(s, ((0, 0), (1, 0), (0, 0)))[:, :-1]
            return jnp.concatenate([a, s], -1)

        def l2norm(t):
            return t / jnp.maximum(jnp.linalg.norm(t, axis=-1, keepdims=True), 1e-12)

        def rotate_half(x):
            x1, x2 = jnp.split(x, 2, -1)
            return jnp.concatenate([-x2, x1], -1)

        def rotary_tables(n):
            half = jnp.arange(0, DIM_HEAD, 2, dtype=jnp.float32)
            inv_freq = 1.0 / 10000.0 ** (half / DIM_HEAD)
            t = jnp.arange(n, dtype=jnp.float32)
            freqs = t[:, None] * inv_freq[None, :]
            freqs = jnp.concatenate([freqs, freqs], -1)
            base_scale = (half + 0.4 * DIM_HEAD) / (1.4 * DIM_HEAD)
            power = (t - n // 2) / (WINDOW // 2)
            scale = base_scale[None, :] ** power[:, None]
            scale = jnp.concatenate([scale, scale], -1)
            return (freqs, scale)

        def local_attention(q, k, v):
            b, h, n, d = q.shape
            w = WINDOW
            nw = n // w
            bq = q.reshape(b, h, nw, w, d)
            bk = k.reshape(b, h, nw, w, d)
            bv = v.reshape(b, h, nw, w, d)

            def look(t):
                p = jnp.pad(t, ((0, 0), (0, 0), (1, 0), (0, 0), (0, 0)))
                return jnp.concatenate([p[:, :, :nw], p[:, :, 1:]], axis=3)
            bk2, bv2 = (look(bk), look(bv))
            seq = jnp.arange(n).reshape(nw, w)
            seq_p = jnp.pad(seq, ((1, 0), (0, 0)), constant_values=-1)
            jt = jnp.concatenate([seq_p[:nw], seq_p[1:]], axis=1)
            it = seq[:, :, None]
            jb = jt[:, None, :]
            mask = (it < jb) | (it > jb + w) | (jb == -1)
            sim = jnp.einsum('bhwie,bhwje->bhwij', bq, bk2) * QK_SCALE
            sim = jnp.where(mask, -jnp.finfo(sim.dtype).max, sim)
            attn = jax.nn.softmax(sim, -1)
            out = jnp.einsum('bhwij,bhwje->bhwie', attn, bv2)
            return out.reshape(b, h, n, d)

        def attn_layer(x, Wqkv, qs, ksc, Wo):
            b, n, _ = x.shape
            qkv = x @ Wqkv
            q, k, v = jnp.split(qkv, 3, -1)
            sh = lambda t: t.reshape(b, n, HEADS, DIM_HEAD).transpose(0, 2, 1, 3)
            q, k, v = (sh(q), sh(k), sh(v))
            q = l2norm(q) * qs
            k = l2norm(k) * ksc
            freqs, scale = rotary_tables(n)
            cos, sin = (jnp.cos(freqs), jnp.sin(freqs))
            q = q * cos * scale + rotate_half(q) * sin * scale
            inv = 1.0 / scale
            k = k * cos * inv + rotate_half(k) * sin * inv
            out = local_attention(q, k, v)
            out = out.transpose(0, 2, 1, 3).reshape(b, n, INNER)
            return out @ Wo

        def ffn_layer(x, g, bln, W1, b1, W2, b2):
            mu = x.mean(-1, keepdims=True)
            var = ((x - mu) ** 2).mean(-1, keepdims=True)
            xn = (x - mu) / jnp.sqrt(var + 1e-05) * g + bln
            hg = xn @ W1 + b1
            a, gate = jnp.split(hg, 2, -1)
            return a * jax.nn.gelu(gate, approximate=False) @ W2 + b2
        key = jax.random.key(seed)
        ks = jax.random.split(key, 8)
        B, N = (2, 256)
        init = lambda k, shape: jax.random.normal(k, shape, jnp.float32) * 0.02
        return {'x': jax.random.normal(ks[0], (B, N, DIM), jnp.float32), 'Wqkv': init(ks[1], (DEPTH, DIM, 3 * INNER)), 'q_scale': jnp.ones((DEPTH, DIM_HEAD), jnp.float32), 'k_scale': jnp.ones((DEPTH, DIM_HEAD), jnp.float32), 'Wo': init(ks[2], (DEPTH, INNER, DIM)), 'ln_g': jnp.ones((DEPTH, DIM), jnp.float32), 'ln_b': jnp.zeros((DEPTH, DIM), jnp.float32), 'W1': init(ks[3], (DEPTH, DIM, 2 * DIM_INNER)), 'b1': jnp.zeros((DEPTH, 2 * DIM_INNER), jnp.float32), 'W2': init(ks[4], (DEPTH, DIM_INNER, DIM)), 'b2': jnp.zeros((DEPTH, DIM), jnp.float32)}
    _L0_ffn_all = _L0_ffn_setup()
    _L0_ffn_in = {k: v for k, v in _L0_ffn_all.items() if k in ('Wqkv', 'q_scale', 'k_scale', 'Wo', 'ln_g', 'ln_b', 'W1', 'b1', 'W2', 'b2')}
    del _L0_ffn_all

    def _L1_xattn_setup():
        import jax, jax.numpy as jnp
        import numpy as np
        NUM_HEADS = 16
        D_MODEL = 128
        D_K = 64
        D_V = 64
        NEG_INF = -1000000000.0
        key = jax.random.key(seed)
        ks = jax.random.split(key, 7)
        B, S = (2, 256)
        Q = jax.random.normal(ks[0], (B, S, D_MODEL), dtype=jnp.float32)
        K = jax.random.normal(ks[1], (B, S, D_MODEL), dtype=jnp.float32)
        V = jax.random.normal(ks[2], (B, S, D_MODEL), dtype=jnp.float32)
        s = 1.0 / np.sqrt(D_MODEL)
        W_q = jax.random.normal(ks[3], (D_MODEL, D_K * NUM_HEADS), dtype=jnp.float32) * s
        W_k = jax.random.normal(ks[4], (D_MODEL, D_K), dtype=jnp.float32) * s
        W_v = jax.random.normal(ks[5], (D_MODEL, D_V), dtype=jnp.float32) * s
        W_o = jax.random.normal(ks[6], (D_V * NUM_HEADS, D_MODEL), dtype=jnp.float32) * (1.0 / np.sqrt(D_V * NUM_HEADS))
        return {'Q': Q, 'K': K, 'V': V, 'W_q': W_q, 'W_k': W_k, 'W_v': W_v, 'W_o': W_o}
    _L1_xattn_all = _L1_xattn_setup()
    _L1_xattn_in = {k: v for k, v in _L1_xattn_all.items() if k in ('W_q', 'W_k', 'W_v', 'W_o')}
    del _L1_xattn_all

    def _L1_ffn_setup():
        import jax, jax.numpy as jnp
        import numpy as np
        B, S, H, F, E, R, TOPK = (4, 256, 128, 512, 4, 4, 2)

        def _more_forward(x, Wg, bg, W1, b1, W2, b2):
            b, s, h = x.shape
            cur = x
            for r in range(R):
                flat = cur.reshape(-1, h)
                logits = flat @ Wg[r] + bg[r]
                vals, idx = jax.lax.top_k(logits, TOPK)
                w = jax.nn.softmax(vals, axis=-1)
                cw = jnp.sum(jax.nn.one_hot(idx, E, dtype=flat.dtype) * w[..., None], axis=1)
                hmid = jax.nn.gelu(jnp.einsum('nh,ehf->enf', flat, W1) + b1[:, None, :])
                y = jnp.einsum('enf,efh->enh', hmid, W2) + b2[:, None, :]
                out = jnp.einsum('ne,enh->nh', cw, y)
                cur = cur + out.reshape(b, s, h)
            return cur
        key = jax.random.key(seed)
        ks = jax.random.split(key, 8)
        scale = 0.02
        return {'x': jax.random.normal(ks[0], (B, S, H), dtype=jnp.float32), 'Wg': jax.random.normal(ks[1], (R, H, E), dtype=jnp.float32) * scale, 'bg': jnp.zeros((R, E), dtype=jnp.float32), 'W1': jax.random.normal(ks[2], (E, H, F), dtype=jnp.float32) * scale, 'b1': jnp.zeros((E, F), dtype=jnp.float32), 'W2': jax.random.normal(ks[3], (E, F, H), dtype=jnp.float32) * scale, 'b2': jnp.zeros((E, H), dtype=jnp.float32)}
    _L1_ffn_all = _L1_ffn_setup()
    _L1_ffn_in = {k: v for k, v in _L1_ffn_all.items() if k in ('Wg', 'bg', 'W1', 'b1', 'W2', 'b2')}
    del _L1_ffn_all
    return {'x': x, 'ctx_1024': ctx_1024, 'mask_Bx1x1xS2_bf1': mask_Bx1x1xS2_bf1, 'L0_xattn_w_q': _L0_xattn_in['w_q'], 'L0_xattn_b_q': _L0_xattn_in['b_q'], 'L0_xattn_w_k': _L0_xattn_in['w_k'], 'L0_xattn_b_k': _L0_xattn_in['b_k'], 'L0_xattn_w_v': _L0_xattn_in['w_v'], 'L0_xattn_b_v': _L0_xattn_in['b_v'], 'L0_xattn_w_o': _L0_xattn_in['w_o'], 'L0_xattn_b_o': _L0_xattn_in['b_o'], 'L0_ffn_Wqkv': _L0_ffn_in['Wqkv'], 'L0_ffn_q_scale': _L0_ffn_in['q_scale'], 'L0_ffn_k_scale': _L0_ffn_in['k_scale'], 'L0_ffn_Wo': _L0_ffn_in['Wo'], 'L0_ffn_ln_g': _L0_ffn_in['ln_g'], 'L0_ffn_ln_b': _L0_ffn_in['ln_b'], 'L0_ffn_W1': _L0_ffn_in['W1'], 'L0_ffn_b1': _L0_ffn_in['b1'], 'L0_ffn_W2': _L0_ffn_in['W2'], 'L0_ffn_b2': _L0_ffn_in['b2'], 'L1_xattn_W_q': _L1_xattn_in['W_q'], 'L1_xattn_W_k': _L1_xattn_in['W_k'], 'L1_xattn_W_v': _L1_xattn_in['W_v'], 'L1_xattn_W_o': _L1_xattn_in['W_o'], 'L1_ffn_Wg': _L1_ffn_in['Wg'], 'L1_ffn_bg': _L1_ffn_in['bg'], 'L1_ffn_W1': _L1_ffn_in['W1'], 'L1_ffn_b1': _L1_ffn_in['b1'], 'L1_ffn_W2': _L1_ffn_in['W2'], 'L1_ffn_b2': _L1_ffn_in['b2']}

def reference(x, ctx_1024, mask_Bx1x1xS2_bf1, L0_xattn_w_q, L0_xattn_b_q, L0_xattn_w_k, L0_xattn_b_k, L0_xattn_w_v, L0_xattn_b_v, L0_xattn_w_o, L0_xattn_b_o, L0_ffn_Wqkv, L0_ffn_q_scale, L0_ffn_k_scale, L0_ffn_Wo, L0_ffn_ln_g, L0_ffn_ln_b, L0_ffn_W1, L0_ffn_b1, L0_ffn_W2, L0_ffn_b2, L1_xattn_W_q, L1_xattn_W_k, L1_xattn_W_v, L1_xattn_W_o, L1_ffn_Wg, L1_ffn_bg, L1_ffn_W1, L1_ffn_b1, L1_ffn_W2, L1_ffn_b2):
    import jax
    import jax.numpy as jnp

    def _L0_xattn_ref(q, k, v, mask, w_q, b_q, w_k, b_k, w_v, b_v, w_o, b_o):
        import jax, jax.numpy as jnp
        import numpy as np
        D_MODEL = 128
        NUM_HEADS = 16
        D_K = D_MODEL // NUM_HEADS
        b, t1, _ = q.shape
        t2 = k.shape[1]
        qh = (q @ w_q.T + b_q).reshape(b, t1, NUM_HEADS, D_K).transpose(0, 2, 1, 3)
        kh = (k @ w_k.T + b_k).reshape(b, t2, NUM_HEADS, D_K).transpose(0, 2, 1, 3)
        vh = (v @ w_v.T + b_v).reshape(b, t2, NUM_HEADS, D_K).transpose(0, 2, 1, 3)
        scores = jnp.einsum('bhqd,bhkd->bhqk', qh, kh) / jnp.sqrt(jnp.asarray(D_K, qh.dtype))
        scores = jnp.where(mask, scores, jnp.asarray(-jnp.inf, scores.dtype))
        attn = jax.nn.softmax(scores, axis=-1)
        out = jnp.einsum('bhqk,bhkd->bhqd', attn, vh)
        out = out.transpose(0, 2, 1, 3).reshape(b, t1, D_MODEL)
        return out @ w_o.T + b_o

    def _L0_ffn_ref(x, Wqkv, q_scale, k_scale, Wo, ln_g, ln_b, W1, b1, W2, b2):
        import jax, jax.numpy as jnp
        import numpy as np
        DIM = 128
        DEPTH = 6
        HEADS = 16
        DIM_HEAD = 64
        WINDOW = 32
        INNER = HEADS * DIM_HEAD
        DIM_INNER = int(DIM * 4 * 2 / 3)
        QK_SCALE = 8.0

        def shift_tokens(t):
            a, s = jnp.split(t, 2, -1)
            s = jnp.pad(s, ((0, 0), (1, 0), (0, 0)))[:, :-1]
            return jnp.concatenate([a, s], -1)

        def l2norm(t):
            return t / jnp.maximum(jnp.linalg.norm(t, axis=-1, keepdims=True), 1e-12)

        def rotate_half(x):
            x1, x2 = jnp.split(x, 2, -1)
            return jnp.concatenate([-x2, x1], -1)

        def rotary_tables(n):
            half = jnp.arange(0, DIM_HEAD, 2, dtype=jnp.float32)
            inv_freq = 1.0 / 10000.0 ** (half / DIM_HEAD)
            t = jnp.arange(n, dtype=jnp.float32)
            freqs = t[:, None] * inv_freq[None, :]
            freqs = jnp.concatenate([freqs, freqs], -1)
            base_scale = (half + 0.4 * DIM_HEAD) / (1.4 * DIM_HEAD)
            power = (t - n // 2) / (WINDOW // 2)
            scale = base_scale[None, :] ** power[:, None]
            scale = jnp.concatenate([scale, scale], -1)
            return (freqs, scale)

        def local_attention(q, k, v):
            b, h, n, d = q.shape
            w = WINDOW
            nw = n // w
            bq = q.reshape(b, h, nw, w, d)
            bk = k.reshape(b, h, nw, w, d)
            bv = v.reshape(b, h, nw, w, d)

            def look(t):
                p = jnp.pad(t, ((0, 0), (0, 0), (1, 0), (0, 0), (0, 0)))
                return jnp.concatenate([p[:, :, :nw], p[:, :, 1:]], axis=3)
            bk2, bv2 = (look(bk), look(bv))
            seq = jnp.arange(n).reshape(nw, w)
            seq_p = jnp.pad(seq, ((1, 0), (0, 0)), constant_values=-1)
            jt = jnp.concatenate([seq_p[:nw], seq_p[1:]], axis=1)
            it = seq[:, :, None]
            jb = jt[:, None, :]
            mask = (it < jb) | (it > jb + w) | (jb == -1)
            sim = jnp.einsum('bhwie,bhwje->bhwij', bq, bk2) * QK_SCALE
            sim = jnp.where(mask, -jnp.finfo(sim.dtype).max, sim)
            attn = jax.nn.softmax(sim, -1)
            out = jnp.einsum('bhwij,bhwje->bhwie', attn, bv2)
            return out.reshape(b, h, n, d)

        def attn_layer(x, Wqkv, qs, ksc, Wo):
            b, n, _ = x.shape
            qkv = x @ Wqkv
            q, k, v = jnp.split(qkv, 3, -1)
            sh = lambda t: t.reshape(b, n, HEADS, DIM_HEAD).transpose(0, 2, 1, 3)
            q, k, v = (sh(q), sh(k), sh(v))
            q = l2norm(q) * qs
            k = l2norm(k) * ksc
            freqs, scale = rotary_tables(n)
            cos, sin = (jnp.cos(freqs), jnp.sin(freqs))
            q = q * cos * scale + rotate_half(q) * sin * scale
            inv = 1.0 / scale
            k = k * cos * inv + rotate_half(k) * sin * inv
            out = local_attention(q, k, v)
            out = out.transpose(0, 2, 1, 3).reshape(b, n, INNER)
            return out @ Wo

        def ffn_layer(x, g, bln, W1, b1, W2, b2):
            mu = x.mean(-1, keepdims=True)
            var = ((x - mu) ** 2).mean(-1, keepdims=True)
            xn = (x - mu) / jnp.sqrt(var + 1e-05) * g + bln
            hg = xn @ W1 + b1
            a, gate = jnp.split(hg, 2, -1)
            return a * jax.nn.gelu(gate, approximate=False) @ W2 + b2
        for i in range(DEPTH):
            x = attn_layer(shift_tokens(x), Wqkv[i], q_scale[i], k_scale[i], Wo[i]) + x
            x = ffn_layer(shift_tokens(x), ln_g[i], ln_b[i], W1[i], b1[i], W2[i], b2[i]) + x
        return x

    def _L1_xattn_ref(Q, K, V, W_q, W_k, W_v, W_o):
        import jax, jax.numpy as jnp
        import numpy as np
        NUM_HEADS = 16
        D_MODEL = 128
        D_K = 64
        D_V = 64
        NEG_INF = -1000000000.0
        B, Sq, _ = Q.shape
        Sk = K.shape[1]
        q = (Q @ W_q).reshape(B, Sq, NUM_HEADS, D_K).transpose(0, 2, 1, 3)
        k = K @ W_k
        v = V @ W_v
        scores = jnp.einsum('bhqd,bkd->bhqk', q, k) / jnp.sqrt(jnp.float32(D_K))
        causal = jnp.tril(jnp.ones((Sq, Sk), dtype=bool))
        scores = jnp.where(causal[None, None], scores, NEG_INF)
        attn = jax.nn.softmax(scores, axis=-1)
        out = jnp.einsum('bhqk,bkd->bhqd', attn, v)
        out = out.transpose(0, 2, 1, 3).reshape(B, Sq, NUM_HEADS * D_V)
        return out @ W_o

    def _L1_ffn_ref(x, Wg, bg, W1, b1, W2, b2):
        import jax, jax.numpy as jnp
        import numpy as np
        B, S, H, F, E, R, TOPK = (4, 256, 128, 512, 4, 4, 2)

        def _more_forward(x, Wg, bg, W1, b1, W2, b2):
            b, s, h = x.shape
            cur = x
            for r in range(R):
                flat = cur.reshape(-1, h)
                logits = flat @ Wg[r] + bg[r]
                vals, idx = jax.lax.top_k(logits, TOPK)
                w = jax.nn.softmax(vals, axis=-1)
                cw = jnp.sum(jax.nn.one_hot(idx, E, dtype=flat.dtype) * w[..., None], axis=1)
                hmid = jax.nn.gelu(jnp.einsum('nh,ehf->enf', flat, W1) + b1[:, None, :])
                y = jnp.einsum('enf,efh->enh', hmid, W2) + b2[:, None, :]
                out = jnp.einsum('ne,enh->nh', cw, y)
                cur = cur + out.reshape(b, s, h)
            return cur
        return _more_forward(x, Wg, bg, W1, b1, W2, b2)
    x = x + _L0_xattn_ref(_layernorm(x, axis=-1), ctx_1024, ctx_1024, mask_Bx1x1xS2_bf1, L0_xattn_w_q, L0_xattn_b_q, L0_xattn_w_k, L0_xattn_b_k, L0_xattn_w_v, L0_xattn_b_v, L0_xattn_w_o, L0_xattn_b_o)
    x = x + _L0_ffn_ref(_layernorm(x, axis=-1), L0_ffn_Wqkv, L0_ffn_q_scale, L0_ffn_k_scale, L0_ffn_Wo, L0_ffn_ln_g, L0_ffn_ln_b, L0_ffn_W1, L0_ffn_b1, L0_ffn_W2, L0_ffn_b2)
    x = x + _L1_xattn_ref(_layernorm(x, axis=-1), ctx_1024, ctx_1024, L1_xattn_W_q, L1_xattn_W_k, L1_xattn_W_v, L1_xattn_W_o)
    x = x + _L1_ffn_ref(_layernorm(x, axis=-1), L1_ffn_Wg, L1_ffn_bg, L1_ffn_W1, L1_ffn_b1, L1_ffn_W2, L1_ffn_b2)
    return x

_drawn_inputs = setup_inputs


def setup_inputs(seed=0):
    import zlib

    import numpy as np

    out = dict(_drawn_inputs(seed))
    spreads = {'L0_ffn_q_scale': (1.0, 0.6),
     'L0_ffn_k_scale': (1.0, 0.6),
     'L0_ffn_ln_g': (1.0, 0.6),
     'L0_ffn_ln_b': (0.0, 0.8),
     'L0_ffn_b1': (0.0, 0.8),
     'L0_ffn_b2': (0.0, 0.1),
     'L1_ffn_bg': (0.0, 0.408),
     'L1_ffn_b1': (0.0, 0.429),
     'L1_ffn_b2': (0.0, 0.271)}
    factors = {'L0_xattn_b_q': 2.917,
     'L0_xattn_b_k': 64.0,
     'L0_ffn_W1': 3.791,
     'L0_ffn_W2': 3.72,
     'L1_ffn_W1': 3.074}
    for name, (base, spread) in spreads.items():
        noise = np.random.default_rng([zlib.crc32(name.encode()), seed]).standard_normal(out[name].shape)
        drawn = base * np.exp(spread * noise) if base else spread * noise
        out[name] = jnp.asarray(drawn.astype(out[name].dtype))
    for name, factor in factors.items():
        out[name] = (out[name] * factor).astype(out[name].dtype)
    return out
```

```python
from contextlib import ExitStack

import concourse.bass as bass
from concourse import mybir
import numpy as np

F32 = mybir.dt.float32
I32 = mybir.dt.int32
ALU = mybir.AluOpType
ACT = mybir.ActivationFunctionType
X = mybir.AxisListType.X

P = 128
B, S = 4, 512
NT = S // P
H = 16
SK = 77
DEPTH = 6
DH = 64
W = 32
FI = 341
FCH = [(0, 128), (128, 128), (256, FI - 256)]
UNITS = DEPTH * B
E, R, FF = 4, 4, 512
NEG = -3.0e38
EPS = 1e-5
HJ = [(0, 6), (6, 6), (12, 4)]
MAGIC = 0x5F3759DF


def constants():
    f = np.float32
    half = np.arange(0, DH, 2, dtype=f)
    inv_freq = (f(1.0) / np.power(f(10000.0), half / f(DH))).astype(f)
    t = np.arange(S, dtype=f)
    freqs = t[:, None] * inv_freq[None, :]
    freqs = np.concatenate([freqs, freqs], -1)
    base = ((half + f(0.4 * DH)) / f(1.4 * DH)).astype(f)
    scale = np.power(base[None, :], ((t - S // 2) / f(W // 2))[:, None]).astype(f)
    scale = np.concatenate([scale, scale], -1)
    sign = np.where(np.arange(DH) < DH // 2, -1.0, 1.0).astype(f)
    cos, sin = np.cos(freqs), np.sin(freqs) * sign
    rot = np.zeros((P, 2, 2, NT, DH), f)
    for qk, m in enumerate((scale * f(8.0), f(1.0) / scale)):
        for cs, w in enumerate((cos, sin)):
            rot[:, qk, cs] = (w * m).reshape(NT, P, DH).transpose(1, 0, 2)
    q, k = np.arange(P)[:, None], np.arange(P)[None, :]
    band = np.where((k <= q) & (q - k <= W), 0.0, NEG).astype(f)
    back = np.zeros((P, W), f)
    back[:W] = np.where(np.arange(W)[None, :] >= np.arange(W)[:, None], 0.0, NEG)
    tok = np.arange(S).reshape(NT, P).T
    causal = np.where(tok[:, :, None] >= np.arange(SK), 0.0, NEG).astype(f)
    heads8 = (np.arange(P)[:, None] // 8 == np.arange(H)[None]).astype(f)
    halves = (np.arange(P)[:, None] // DH == np.arange(2)[None]).astype(f)
    before = np.broadcast_to((np.arange(E)[None, :] < np.arange(E)[:, None]), (P, E, E)).astype(f)
    parts = dict(ident=np.eye(P, dtype=f), rot=rot, band=band, back=back, causal=causal,
                 heads8=heads8, halves=halves, before=before)
    place, at = {}, 0
    for n, a in parts.items():
        place[n] = (at, a.size // P)
        at += a.size // P
    return np.concatenate([a.reshape(P, -1) for a in parts.values()], 1), place


class Ring:

    def __init__(self, ctx, nc, name, banks, first, steady):
        self.banks = banks
        n = len(banks)
        assert first % n == 0 and steady % n == 0
        self.first, self.steady = first, steady
        self.full = [ctx.enter_context(nc.semaphore(f"{name}_full{i}")) for i in range(n)]
        self.free = [ctx.enter_context(nc.semaphore(f"{name}_free{i}")) for i in range(n)]

    def cursor(self):
        return Cursor(self)


class Cursor:
    def __init__(self, ring):
        self.ring, self.n, self.i = ring, 0, 0

    def begin(self, i):
        self.i, self.n = i, 0

    def end(self):
        first = isinstance(self.i, int) and self.i == 0
        assert self.n == (self.ring.first if first else self.ring.steady), (self.n, first)

    def next(self):
        r = self.ring
        nb = len(r.banks)
        k = self.n % nb
        q = self.n // nb
        if not (isinstance(self.i, int) and self.i == 0):
            q = self.i * (r.steady // nb) + (r.first // nb - r.steady // nb + q)
        self.n += 1
        return r.banks[k], q, r.full[k], r.free[k]


class Chain:

    def __init__(self, eng, sem, first, steady):
        self.eng, self.sem, self.first, self.steady, self.n, self.base = eng, sem, first, steady, 0, 0

    def begin(self, i):
        self.n = 0
        self.base = 0 if isinstance(i, int) and i == 0 else i * self.steady + (self.first - self.steady)

    def end(self):
        want = self.first if isinstance(self.base, int) and self.base == 0 else self.steady
        assert self.n == want, (self.n, want)

    def link(self, ins):
        self.n += 1
        ins.then_inc(self.sem, 1)
        self.eng.wait_ge(self.sem, self.base + self.n)


def wait(eng, sem, value):
    if isinstance(value, int) and value <= 0:
        return
    eng.wait_ge(sem, value)


def experts(nc, ctx, o):
    sb, sem, ins, psum, xT, yT, ident, table = (o[k] for k in ("sb", "sem", "ins", "psum", "xT", "yT", "ident", "table"))
    FC = FF // P
    with ExitStack() as c:
        w1 = sb("moe_w1", [P, E, FF], c)
        w2 = sb("moe_w2", [P, E, FC, P], c)
        b1 = sb("moe_b1", [P, E, FC], c)
        b2 = sb("moe_b2", [E, P], c)
        wg = sb("moe_wg", [P, R, E], c)
        bg = sb("moe_bg", [P, R, E], c)
        hm = sb("moe_hidden", [P, 2, FC, S], c)
        lg, sl, z, sel, cw = (sb(f"moe_{n}", [P, NT, E], c) for n in ("logits", "chosen_logits", "z", "chosen", "weights"))
        th = sb("moe_tanh", [P, NT, E], c)
        gt, ge = sb("moe_gt", [P, NT, E, E], c), sb("moe_ge", [P, NT, E, E], c)
        rank, tot = sb("moe_rank", [P, NT, E], c), sb("moe_total", [P, NT], c)
        cwT = sb("moe_weightsT", [E, S], c)
        acc = sb("moe_acc", [P, NT, P], c)
        w_in = sem("moe_w_in", c)
        z_done, th_done, cw_done = sem("z_done", c), sem("th_done", c), sem("cw_done", c)
        y_done, self_v = sem("y_done", c), sem("moe_self_v", c)
        gate = Ring(c, nc, "gate", [psum[0]], 2 * B, 2 * B)
        hid = Ring(c, nc, "hid", psum[1:5], E * FC * B, E * FC * B)
        ye = Ring(c, nc, "ye", psum[5:7], E * B, E * B)
        dl = Ring(c, nc, "dl", [psum[7]], B, B)
        block = c.enter_context(nc.Block())

        @block.sync
        def _(sp):
            sp.dma_start(wg[:, :, :], ins["L1_ffn_Wg"].rearrange("r h e -> h r e")).then_inc(w_in, 16)
            sp.dma_start(bg[:, :, :], ins["L1_ffn_bg"].rearrange("(o r) e -> o r e", o=1).broadcast_to([P, R, E]))\
                .then_inc(w_in, 16)
            sp.dma_start(w1[:, :, :], ins["L1_ffn_W1"].rearrange("e h f -> h e f")).then_inc(w_in, 16)
            sp.dma_start(b1[:, :, :], ins["L1_ffn_b1"]).then_inc(w_in, 16)
            sp.dma_start(w2[:, :, :, :], ins["L1_ffn_W2"].rearrange("e (c p) h -> p e c h", p=P)).then_inc(w_in, 16)
            sp.dma_start(b2[:, :], ins["L1_ffn_b2"]).then_inc(w_in, 16)

        @block.tensor
        def _(pe):
            gate_c, hid_c, ye_c, dl_c = gate.cursor(), hid.cursor(), ye.cursor(), dl.cursor()

            def unit(r, b):
                i = r * B + b
                y = yT[:, b, 1:S + 1]
                if not (isinstance(r, int) and r == 0):
                    pe.wait_ge(y_done, i - B + 1)
                bank, q, full, free = gate_c.next()
                wait(pe, free, q)
                for t in range(NT):
                    last = nc.tensor.matmul(bank[:, t * E:(t + 1) * E], yT[:, b, 1 + t * P:1 + (t + 1) * P],
                                            wg[:, bass.ds(r, 1), :].rearrange("p o e -> p (o e)"), start=True, stop=True)
                last.then_inc(full, 1)
                moved = {}

                def hidden(e):
                    for f in range(FC):
                        bank, q, full, free = hid_c.next()
                        wait(pe, free, q)
                        nc.tensor.matmul(bank[:, :], w1[:, e, f * P:(f + 1) * P], y, start=True, stop=True)\
                            .then_inc(full, 1)
                        moved[e, f] = (free, q + 1)

                def outputs(e):
                    bank, q, full, free = ye_c.next()
                    for f in range(FC):
                        pe.wait_ge(*moved[e, f])
                    wait(pe, free, q)
                    for t in range(NT):
                        for f in range(FC):
                            last = nc.tensor.matmul(bank[:, t * P:(t + 1) * P], hm[:, e % 2, f, t * P:(t + 1) * P],
                                                    w2[:, e, f, :], start=(f == 0), stop=(f == FC - 1))
                    last.then_inc(full, 1)
                    return free, q + 1

                hidden(0)
                hidden(1)
                bank, q, full, free = gate_c.next()
                pe.wait_ge(cw_done, i + 1)
                for t in range(NT):
                    last = nc.tensor.transpose(bank[0:E, t * P:(t + 1) * P], cw[:, t, :], ident)
                last.then_inc(full, 1)
                weights = (free, q + 1)
                outputs(0)
                hidden(2)
                outputs(1)
                hidden(3)
                outputs(2)
                summed = outputs(3)
                bank, q, full, free = dl_c.next()
                wait(pe, y_done, i)
                pe.wait_ge(*weights)
                nc.tensor.matmul(bank[:, :], b2[:, :], cwT[:, :], start=True, stop=False, skip_group_check=True)
                pe.wait_ge(*summed)
                for t in range(NT):
                    last = nc.tensor.matmul(bank[:, t * P:(t + 1) * P], acc[:, t, :], ident, start=False,
                                            stop=(t == NT - 1), skip_group_check=True)
                last.then_inc(full, 1)

            def body(r):
                for cur in (gate_c, hid_c, ye_c, dl_c):
                    cur.begin(r)
                for b in range(B):
                    unit(r, b)
                for cur in (gate_c, hid_c, ye_c, dl_c):
                    cur.end()

            pe.wait_ge(w_in, 6 * 16)
            body(0)
            with pe.Fori(1, R) as r:
                body(r)

        @block.scalar
        def _(act):
            gate_c, hid_c, ye_c = gate.cursor(), hid.cursor(), ye.cursor()

            def unit(r, b):
                i = r * B + b
                gate_c.next()

                def hidden(e):
                    _, q, full, _ = ye_c.next()
                    wait(act, full, q)
                    for f in range(FC):
                        bank, q, full, free = hid_c.next()
                        act.wait_ge(full, q + 1)
                        nc.scalar.activation(hm[:, e % 2, f, :], bank[:, :], ACT.Gelu_apprx_tanh,
                                             bias=b1[:, e, f:f + 1]).then_inc(free, 1)

                hidden(0)
                act.wait_ge(z_done, i + 1)
                nc.scalar.activation(th[:, :, :], z[:, :, :], ACT.Tanh).then_inc(th_done, 1)
                hidden(1)
                bank, q, full, free = gate_c.next()
                act.wait_ge(full, q + 1)
                wait(act, y_done, i)
                nc.scalar.activation(cwT[:, :], bank[0:E, :], ACT.Copy).then_inc(free, 1)
                hidden(2)
                hidden(3)

            def body(r):
                for cur in (gate_c, hid_c, ye_c):
                    cur.begin(r)
                for b in range(B):
                    unit(r, b)
                for cur in (gate_c, hid_c, ye_c):
                    cur.end()

            act.wait_ge(w_in, 6 * 16)
            body(0)
            with act.Fori(1, R) as r:
                body(r)

        @block.vector
        def _(dve):
            LINKS = 9 * B
            chain = Chain(dve, self_v, LINKS, LINKS)
            gate_c, ye_c, dl_c = gate.cursor(), ye.cursor(), dl.cursor()

            def unit(r, b):
                i = r * B + b
                bank, q, full, free = gate_c.next()
                dve.wait_ge(full, q + 1)
                wait(dve, y_done, i)
                v = nc.vector
                v.tensor_tensor(lg[:, :, :], bank[:, 0:NT * E].rearrange("p (t e) -> p t e", e=E),
                                bg[:, bass.ds(r, 1), :].broadcast_to([P, NT, E]), ALU.add).then_inc(free, 1)
                dve.wait_ge(free, q + 1)
                mine = lg[:, :, :].unsqueeze(3).broadcast_to([P, NT, E, E])
                other = lg[:, :, :].unsqueeze(2).broadcast_to([P, NT, E, E])
                v.tensor_tensor(ge[:, :, :, :], other, mine, ALU.is_ge)
                chain.link(v.tensor_tensor(gt[:, :, :, :], other, mine, ALU.is_gt))
                chain.link(v.tensor_tensor(ge[:, :, :, :], ge[:, :, :, :], gt[:, :, :, :], ALU.subtract))
                first = table("before").rearrange("p (e f) -> p e f", f=E).unsqueeze(1).broadcast_to([P, NT, E, E])
                chain.link(v.tensor_tensor(ge[:, :, :, :], ge[:, :, :, :], first, ALU.mult))
                chain.link(v.tensor_tensor(ge[:, :, :, :], ge[:, :, :, :], gt[:, :, :, :], ALU.add))
                chain.link(v.tensor_reduce(rank[:, :, :], ge[:, :, :, :], X, ALU.add))
                chain.link(v.tensor_scalar(sel[:, :, :], rank[:, :, :], 1.5, None, ALU.is_lt))
                chain.link(v.tensor_tensor(sl[:, :, :], sel[:, :, :], lg[:, :, :], ALU.mult))
                chain.link(v.tensor_reduce(tot[:, :], sl[:, :, :], X, ALU.add))
                v.scalar_tensor_tensor(out=z[:, :, :], in0=tot[:, :].unsqueeze(2).broadcast_to([P, NT, E]), scalar=-0.5,
                                       in1=lg[:, :, :], op0=ALU.mult, op1=ALU.add).then_inc(z_done, 1)
                dve.wait_ge(th_done, i + 1)
                chain.link(v.scalar_tensor_tensor(out=th[:, :, :], in0=th[:, :, :], scalar=1.0, in1=sel[:, :, :],
                                                  op0=ALU.add, op1=ALU.mult))
                v.tensor_scalar(cw[:, :, :], th[:, :, :], 0.5, None, ALU.mult).then_inc(cw_done, 1)
                dve.wait_ge(cw_done, i + 1)
                gate_c.next()
                for e in range(E):
                    bank, q, full, free = ye_c.next()
                    dve.wait_ge(full, q + 1)
                    for t in range(NT):
                        y = bank[:, t * P:(t + 1) * P]
                        if e == 0:
                            last = v.tensor_scalar(acc[:, t, :], y, cw[:, t, e:e + 1], None, ALU.mult)
                        else:
                            last = v.scalar_tensor_tensor(out=acc[:, t, :], in0=y, scalar=cw[:, t, e:e + 1],
                                                          in1=acc[:, t, :], op0=ALU.mult, op1=ALU.add)
                    last.then_inc(free, 1)
                    dve.wait_ge(free, q + 1)
                bank, q, full, free = dl_c.next()
                dve.wait_ge(full, q + 1)
                ys = yT[:, b, 1:S + 1]
                v.tensor_tensor(ys, bank[:, :], ys, ALU.add).then_inc(y_done, 1)

            def body(r):
                chain.begin(r)
                for cur in (gate_c, ye_c, dl_c):
                    cur.begin(r)
                for b in range(B):
                    unit(r, b)
                chain.end()
                for cur in (gate_c, ye_c, dl_c):
                    cur.end()

            dve.wait_ge(w_in, 6 * 16)
            body(0)
            with dve.Fori(1, R) as r:
                body(r)
            dve.wait_ge(y_done, R * B)
            for b in range(B):
                nc.vector.tensor_tensor(xT[:, b, :], yT[:, b, 1:S + 1], xT[:, b, :], ALU.add)


def local(nc, ctx, o):
    sb, sem, ins, psum, xT, yT, ident, table, ones, mean_w = (
        o[k] for k in ("sb", "sem", "ins", "psum", "xT", "yT", "ident", "table", "ones", "mean_w"))
    with ExitStack() as c:
        def b_(n, shape, dt=F32):
            return sb("loc_" + n, shape, c, dt)

        def s_(n):
            return sem("loc_" + n, c)

        wqkv = b_("wqkv", [P, 2, 3 * H * DH])
        wo = b_("wo", [P, 8, P])
        w1 = b_("w1", [P, 2 * FI])
        w2 = b_("w2", [P, 3, P])
        scales = b_("scales", [P, DEPTH, 2, DH])
        tab = b_("tab", [P, DEPTH, 2, 2, NT, DH])
        vecs = b_("vecs", [P, 3, DEPTH])
        b1 = b_("b1", [P, DEPTH, 2, 3])
        xs = b_("xs", [P, 2, P])
        sq = b_("sq", [P, 2, 512])
        t2 = b_("t2", [P, 4, 8, DH])
        ss = b_("ss", [P, 4, 8])
        yi, na = b_("yi", [P, 4, 8]), b_("na", [P, 4, 8])
        rn = b_("rn", [P, 2, 4, 8])
        qk = b_("qk", [P, 2, 4, 512])
        qT = b_("qT", [P, 8, P])
        kT = b_("kT", [P, 2, 8, P])
        V = b_("V", [P, NT, H, DH])
        sm = b_("sm", [P, H, P + W])
        ex = b_("ex", [P, 2, H, P + W])
        mx = b_("mx", [P, H])
        rs, rr = b_("rs", [P, H]), b_("rr", [P, H])
        pT = b_("pT", [P, 4, 4, P])
        pTb = b_("pTb", [P, H, W])
        OT = b_("OT", [P, 8, P])
        s2, d2 = b_("s2", [P, S]), b_("d2", [P, S])
        v2, y2, a2, r2 = (b_(n, [P, NT]) for n in ("v2", "y2", "a2", "r2"))
        xn = b_("xn", [P, S])
        diag = s2[:, :].rearrange("p (t n) -> p t n", t=NT)
        sq2 = xn
        gg = b_("gg", [P, 2, S])
        ag = [s2[:, :], d2[:, :], gg[:, 0, :]]
        tiny = b_("tiny", [P, B + 2])

        c_in = s_("c_in")
        wqkv_in, wo_in, wf_in = s_("wqkv_in"), s_("wo_in"), s_("wf_in")
        ready = s_("ready")
        xs_in, sq_in = s_("xs_in"), s_("sq_in")
        rot_in, rn_in = s_("rot_in"), s_("rn_in")
        qk_in = s_("qk_in")
        mx_in, ex_in = s_("mx_in"), s_("ex_in")
        rr_in, p_in = s_("rr_in"), s_("p_in")
        s2_in, sq2_in, r2_in, xn_in = s_("s2_in"), s_("sq2_in"), s_("r2_in"), s_("xn_in")
        r1_in, xg_in = s_("r1_in"), s_("xg_in")
        back_in = s_("back_in")
        f_done = s_("f_done")
        self_v, self_p = s_("self_v"), s_("self_p")
        proj = Ring(c, nc, "proj", psum[0:2], 24, 32)
        tr = Ring(c, nc, "tr", [psum[2], psum[6]], 20, 32)
        sc = Ring(c, nc, "sc", psum[3:5], 12, 16)
        bk = Ring(c, nc, "bk", [psum[5]], 6, 12)
        pv = Ring(c, nc, "pv", [psum[7]], 6, 14)

        def pv_before(i):
            return pv.first + (i - 1) * pv.steady

        def where(u, j, back):
            return (u, j - back) if j >= back else (u - 1, j - back + NT)

        def has(u, j, back):
            first, last = isinstance(u, int) and u == 0, isinstance(u, int) and u == UNITS
            return not (first and j < back) and not (last and j >= back)

        def steps(curs, engine_step):
            def iteration(u, nsteps=NT, check=True):
                for cur in curs:
                    cur.begin(u)
                for j in range(nsteps):
                    engine_step(u, j)
                if check:
                    for cur in curs:
                        cur.end()
            return iteration

        c1 = ExitStack()
        block = c1.enter_context(nc.Block())

        @block.sync
        def _(sp):
            for i, n in enumerate(("q_scale", "k_scale")):
                sp.dma_start(scales[:, :, i, :], ins["L0_ffn_" + n].rearrange("(o l) d -> o l d", o=1)
                             .broadcast_to([P, DEPTH, DH])).then_inc(c_in, 16)
            for i, n in enumerate(("ln_g", "ln_b", "b2")):
                sp.dma_start(vecs[:, i, :], ins["L0_ffn_" + n]).then_inc(c_in, 16)
            sp.dma_start(b1[:, :, :, :], ins["L0_ffn_b1"]).then_inc(c_in, 16)
            sp.wait_ge(c_in, 6 * 16)

        @block.vector
        def _(dve):
            nc.vector.memset(sm[:, :, P:P + W], NEG)
            dve.wait_ge(c_in, 6 * 16)
            rot = table("rot").rearrange("p (a c j d) -> p a c j d", a=2, c=2, j=NT)
            for a in range(2):
                def of(cs, lo, hi):
                    return rot[:, a, cs, :, lo:hi].unsqueeze(1).broadcast_to([P, DEPTH, NT, hi - lo])

                def by(lo, hi):
                    return scales[:, :, a, lo:hi].unsqueeze(2).broadcast_to([P, DEPTH, NT, hi - lo])
                nc.vector.tensor_tensor(tab[:, :, a, 0, :, :], of(0, 0, DH), by(0, DH), ALU.mult)
                hd = DH // 2
                nc.vector.tensor_tensor(tab[:, :, a, 1, :, 0:hd], of(1, 0, hd), by(hd, DH), ALU.mult)
                nc.vector.tensor_tensor(tab[:, :, a, 1, :, hd:DH], of(1, hd, DH), by(0, hd), ALU.mult)

        c1.close()
        block = c.enter_context(nc.Block())

        @block.sync
        def _(sp):
            def load_qkv(l, half):
                sp.dma_start(wqkv[:, half, :] if isinstance(half, int) else
                             wqkv[:, bass.ds(half, 1), :].rearrange("p o n -> p (o n)"),
                             ins["L0_ffn_Wqkv"][bass.ds(l, 1), :, :].rearrange("o p n -> p (o n)"))\
                    .then_inc(wqkv_in, 16)

            def load_wo(l):
                sp.dma_start(wo[:, :, :], ins["L0_ffn_Wo"][bass.ds(l, 1), :, :]
                             .rearrange("o (c p) n -> p (o c) n", p=P)).then_inc(wo_in, 16)

            def load_ffn(l):
                sp.dma_start(w1[:, :], ins["L0_ffn_W1"][bass.ds(l, 1), :, :].rearrange("o p n -> p (o n)"))\
                    .then_inc(wf_in, 16)
                src = ins["L0_ffn_W2"][bass.ds(l, 1), :, :]
                sp.dma_start(w2[:, 0:2, :], src[:, 0:2 * P, :].rearrange("o (c p) n -> p (o c) n", p=P))\
                    .then_inc(wf_in, 16)
                sp.dma_start(w2[0:FI - 2 * P, 2, :], src[:, 2 * P:FI, :].rearrange("o p n -> p (o n)"))\
                    .then_inc(wf_in, 16)

            def next_layer(l, more):
                if more:
                    sp.wait_ge(sq_in, l * (4 * NT * B) + 1)
                    load_qkv(l + 1, (l + 1) % 2)
                sp.wait_ge(pv.free[0], pv_before(l * B) + 6)
                load_wo(l)
                sp.wait_ge(f_done, l * B + B)
                load_ffn(l)

            load_qkv(0, 0)
            load_wo(0)
            load_ffn(0)
            sp.wait_ge(wqkv_in, 16)
            load_qkv(1, 1)
            with sp.Fori(1, DEPTH - 1) as l:
                next_layer(l, True)
            next_layer(DEPTH - 1, False)

        @block.tensor
        def _(pe):
            pj, tc, scc, bc, pc = proj.cursor(), tr.cursor(), sc.cursor(), bk.cursor(), pv.cursor()
            moved = {}

            def step(u, j):
                A = has(u, j, 0)
                Bm = has(u, j, 1)
                Ck = has(u, j, 2)
                F_ = not (isinstance(u, int) and u == 0)
                um, jm = where(u, j, 1)
                uk, jk = where(u, j, 2)
                n, m, k = u * NT + j, um * NT + jm, uk * NT + jk

                def project(s):
                    if not A:
                        return
                    if s == 0:
                        if j == 0:
                            pe.wait_ge(wqkv_in, (u // B) * 16 + 16)
                        pe.wait_ge(xs_in, 2 * n + 2)
                    at = (s % 2) * H * DH + (s // 2) * 512 if s < 4 else 2 * H * DH + (s - 4) * 512
                    bank, q, full, free = pj.next()
                    wait(pe, free, q)
                    half = (u // B) % 2
                    rhs = wqkv[:, half, at:at + 512] if isinstance(half, int) else \
                        wqkv[:, bass.ds(half, 1), at:at + 512].rearrange("p o n -> p (o n)")
                    nc.tensor.matmul(bank[:, :], xs[:, j % 2, :], rhs, start=True, stop=True).then_inc(full, 1)

                def turn_p(g):
                    if not Ck:
                        return
                    bank, q, full, free = tc.next()
                    pe.wait_ge(p_in, 2 * k + g // 2 + 1)
                    wait(pe, free, q)
                    for i in range(4):
                        last = nc.tensor.transpose(bank[:, i * P:(i + 1) * P], ex[:, jk % 2, 4 * g + i, 0:P], ident)
                    last.then_inc(full, 1)
                    moved["p", g] = (free, q + 1)

                def turn_back(r):
                    if not Ck or jk == 0:
                        return
                    bank, q, full, free = bc.next()
                    pe.wait_ge(p_in, 2 * k + r + 1)
                    wait(pe, free, q)
                    for i in range(8):
                        last = nc.tensor.matmul(bank[P - W:P, i * W:(i + 1) * W], ex[:, jk % 2, 8 * r + i, P:P + W],
                                                ident[:, 0:W], start=True, stop=True)
                    last.then_inc(full, 1)
                    moved["b", r] = (free, q + 1)

                def outputs(r):
                    if not Ck:
                        return
                    bank, q, full, free = pc.next()
                    for e in range(2):
                        pe.wait_ge(*moved["p", 2 * r + e])
                    if jk > 0:
                        pe.wait_ge(*moved["b", r])
                    wait(pe, free, q)
                    for e in range(2):
                        lo, hi = 64 * e, 64 * e + 64
                        for i in range(4):
                            h = 8 * r + 2 * i + e
                            last = nc.tensor.matmul(bank[lo:hi, i * P:(i + 1) * P], V[:, jk, h, :], pT[:, 2 * r + e, i, :],
                                                    start=True, stop=(jk == 0))
                            if jk > 0:
                                last = nc.tensor.matmul(bank[lo:hi, i * P:i * P + W], V[P - W:P, jk - 1, h, :],
                                                        pTb[P - W:P, 8 * r + 4 * e + i, :], start=False, stop=True)
                    last.then_inc(full, 1)
                    moved["o", r] = (free, q + 1)

                def turn_qk(s):
                    if not Bm:
                        return
                    bank, q, full, free = tc.next()
                    pe.wait_ge(qk_in, 4 * m + s + 1)
                    wait(pe, free, q)
                    for i in range(4):
                        last = nc.tensor.transpose(bank[:, i * P:(i + 1) * P], qk[:, jm % 2, s, i * P:(i + 1) * P], ident)
                    last.then_inc(full, 1)
                    moved["q", s] = (free, q + 1)

                def scores(r):
                    if not Bm:
                        return
                    for s in (2 * r, 2 * r + 1):
                        pe.wait_ge(*moved["q", s])
                    jobs = [scc.next() for e in range(2)]

                    def back(e, bank):
                        lo, hi = 64 * e, 64 * e + 64
                        for i in range(4):
                            at = e * P + i * W
                            last = nc.tensor.matmul(bank[0:W, at:at + W], qT[lo:hi, 4 * r + i, 0:W],
                                                    kT[lo:hi, 1 - jm % 2, 4 * r + i, P - W:P], start=True, stop=True)
                        return last

                    if jm > 0:
                        bank, q, full, free = bc.next()
                        wait(pe, free, q)
                    for e in range(2):
                        wait(pe, jobs[e][3], jobs[e][1])
                    for i in range(4):
                        if i == 2 and jm > 0:
                            back(0, bank).then_inc(back_in, 1)
                        if i == 3 and jm > 0:
                            pe.wait_ge(back_in, 2 * (NT - 1) * um + 2 * (jm - 1) + r + 1)
                        for e in range(2):
                            lo, hi = 64 * e, 64 * e + 64
                            last = nc.tensor.matmul(jobs[e][0][:, i * P:(i + 1) * P], qT[lo:hi, 4 * r + i, :],
                                                    kT[lo:hi, jm % 2, 4 * r + i, :], start=True, stop=True)
                            if i == 3:
                                last.then_inc(jobs[e][2], 1)
                    if jm > 0:
                        back(1, bank).then_inc(full, 1)

                def project_out():
                    if not Ck:
                        return
                    if jk == 0:
                        pe.wait_ge(wo_in, (uk // B) * 16 + 16)
                    bank, q, full, free = pc.next()
                    pe.wait_ge(*moved["o", 1])
                    wait(pe, free, q)
                    for cc in range(8):
                        last = nc.tensor.matmul(bank[:, 0:P], wo[:, cc, :], OT[:, cc, :], start=(cc == 0), stop=(cc == 7))
                    last.then_inc(full, 1)

                def ffn_mean():
                    pe.wait_ge(s2_in, 2 * u)
                    bank, q, full, free = pj.next()
                    pe.wait_ge(free, q)
                    nc.tensor.matmul(bank[:, :], mean_w[:, :], s2[:, :], start=True, stop=True).then_inc(full, 1)

                def ffn_var():
                    pe.wait_ge(sq2_in, u)
                    bank, q, full, free = pj.next()
                    pe.wait_ge(free, q)
                    for t in range(NT):
                        last = nc.tensor.matmul(bank[:, t:t + 1], sq2[:, t * P:(t + 1) * P], mean_w[:, 0:1],
                                                start=True, stop=True)
                    last.then_inc(full, 1)

                def ffn_spread():
                    pe.wait_ge(r2_in, u)
                    bank, q, full, free = pc.next()
                    pe.wait_ge(free, q)
                    nc.tensor.matmul(bank[:, :], ones[:, :], diag[:, :, :].rearrange("p t n -> p (t n)"),
                                     start=True, stop=True).then_inc(full, 1)

                def ffn_up(i, part):
                    if i == 0 and part == 1:
                        pe.wait_ge(xn_in, u)
                        pe.wait_ge(wf_in, ((u - 1) // B) * 48 + 48)
                    lo, w = FCH[i]
                    bank, q, full, free = pj.next()
                    pe.wait_ge(free, q)
                    nc.tensor.matmul(bank[0:w, :], w1[:, part * FI + lo:part * FI + lo + w], xn[:, :],
                                     start=True, stop=True).then_inc(full, 1)
                    moved["f", i] = (free, q + 1)

                def ffn_down():
                    bank, q, full, free = pc.next()
                    for i in range(3):
                        pe.wait_ge(*moved["f", i])
                    pe.wait_ge(free, q)
                    for i, (lo, w) in enumerate(FCH):
                        last = nc.tensor.matmul(bank[:, :], w2[0:w, i, :], ag[i][0:w], start=(i == 0), stop=(i == 2))
                    last.then_inc(full, 1)

                up = F_ and j == 3
                project(0)
                project(1)
                turn_qk(0)
                turn_qk(1)
                project(2)
                scores(0)
                if up:
                    ffn_spread()
                project(3)
                turn_qk(2)
                turn_qk(3)
                turn_back(0)
                turn_p(0)
                turn_p(1)
                project(4)
                scores(1)
                if F_ and j == 2:
                    ffn_mean()
                outputs(0)
                project(5)
                if up:
                    ffn_up(0, 1)
                    ffn_up(0, 0)
                turn_p(2)
                turn_back(1)
                turn_p(3)
                if up:
                    ffn_up(1, 1)
                    ffn_up(1, 0)
                outputs(1)
                if F_ and j == 2:
                    ffn_var()
                if up:
                    ffn_up(2, 1)
                    ffn_up(2, 0)
                project_out()
                if up:
                    ffn_down()

            curs = (pj, tc, scc, bc, pc)
            it = steps(curs, step)
            it(0)
            with pe.Fori(1, UNITS) as u:
                it(u)
            it(UNITS, check=False)

        @block.scalar
        def _(act):
            pj, tc, bc, pc = proj.cursor(), tr.cursor(), bk.cursor(), pv.cursor()

            def step(u, j):
                A, Bm, Ck = has(u, j, 0), has(u, j, 1), has(u, j, 2)
                F_ = not (isinstance(u, int) and u == 0)
                um, jm = where(u, j, 1)
                uk, jk = where(u, j, 2)
                n, m, k = u * NT + j, um * NT + jm, uk * NT + jk

                def square(s):
                    if not A:
                        return
                    bank, q, full, free = pj.next()
                    act.wait_ge(full, q + 1)
                    wait(act, rot_in, 4 * n + s - 1)
                    nc.scalar.activation(sq[:, s % 2, :], bank[:, :], ACT.Square).then_inc(sq_in, 1)

                def values(s):
                    if not A:
                        return
                    bank, q, full, free = pj.next()
                    act.wait_ge(full, q + 1)
                    nc.scalar.activation(V[:, j, 8 * s:8 * s + 8, 0:DH], bank[:, :].rearrange("p (h d) -> p h d", d=DH),
                                         ACT.Copy).then_inc(free, 1)

                def move(dst, on=True):
                    if not on:
                        return
                    bank, q, full, free = tc.next()
                    act.wait_ge(full, q + 1)
                    nc.scalar.activation(dst, bank[:, :], ACT.Copy).then_inc(free, 1)

                def move_p(g):
                    move(pT[:, g, :, :].rearrange("p i t -> p (i t)"), Ck)

                def move_back(r):
                    if not Ck or jk == 0:
                        return
                    bank, q, full, free = bc.next()
                    act.wait_ge(full, q + 1)
                    nc.scalar.activation(pTb[P - W:P, 8 * r:8 * r + 8, 0:W],
                                         bank[P - W:P, 0:8 * W].rearrange("p (i t) -> p i t", t=W), ACT.Copy).then_inc(free, 1)

                def move_o(r):
                    if not Ck:
                        return
                    bank, q, full, free = pc.next()
                    act.wait_ge(full, q + 1)
                    nc.scalar.activation(OT[:, 4 * r:4 * r + 4, :].rearrange("p i t -> p (i t)"), bank[:, :], ACT.Copy)\
                        .then_inc(free, 1)

                def move_qk(s):
                    r = s // 2
                    dst = kT[:, jm % 2, 4 * r:4 * r + 4, :] if s % 2 else qT[:, 4 * r:4 * r + 4, :]
                    move(dst.rearrange("p i t -> p (i t)"), Bm)

                def exponentials(r):
                    if not Bm:
                        return
                    w = P + W if jm > 0 else P
                    act.wait_ge(mx_in, 2 * m + r + 1)
                    for i in range(8 * r, 8 * r + 8):
                        last = nc.scalar.activation(ex[:, jm % 2, i, 0:w], sm[:, i, 0:w], ACT.Exp, bias=mx[:, i:i + 1],
                                                    accum_out=rs[:, i:i + 1])
                    last.then_inc(ex_in, 1)

                up = F_ and j == 3

                def ffn_square(job):
                    bank, q, full, free = job
                    act.wait_ge(free, q + 1)
                    nc.scalar.activation(sq2[:, :], d2[:, :], ACT.Square).then_inc(sq2_in, 1)

                def ffn_gelu(i):
                    lo, w = FCH[i]
                    bank, q, full, free = pj.next()
                    act.wait_ge(full, q + 1)
                    if i == 2:
                        act.wait_ge(*gated[0])
                    nc.scalar.activation(gg[0:w, i % 2, :], bank[0:w, :], ACT.Gelu,
                                         bias=b1[0:w, bass.ds((u - 1) // B, 1), 1, i:i + 1].rearrange("p a b -> p (a b)"))\
                        .then_inc(free, 1)
                    _, q, _, free = pj.next()
                    gated[i] = (free, q + 1)

                gated = {}
                square(0)
                square(1)
                move_qk(0)
                move_qk(1)
                square(2)
                square(3)
                move_qk(2)
                move_qk(3)
                if Bm and jm > 0:
                    bc.next()
                move_back(0)
                move_p(0)
                move_p(1)
                values(0)
                exponentials(0)
                if Bm and jm > 0:
                    bc.next()
                if up:
                    pc.next()
                    act.wait_ge(xg_in, u)
                    nc.scalar.activation(xn[:, :], d2[:, :], ACT.Identity,
                                         bias=vecs[:, 1, bass.ds((u - 1) // B, 1)]).then_inc(xn_in, 1)
                if F_ and j == 2:
                    mean_job = pj.next()
                move_o(0)
                values(1)
                if up:
                    ffn_gelu(0)
                move_p(2)
                move_back(1)
                move_p(3)
                if F_ and j == 2:
                    ffn_square(mean_job)
                    pj.next()
                if up:
                    ffn_gelu(1)
                move_o(1)
                if up:
                    ffn_gelu(2)
                if Ck:
                    pc.next()
                if up:
                    pc.next()
                exponentials(1)

            it = steps((pj, tc, bc, pc), step)
            it(0)
            with act.Fori(1, UNITS) as u:
                it(u)
            it(UNITS, check=False)

        @block.vector
        def _(dve):
            pj, scc, bc, pc = proj.cursor(), sc.cursor(), bk.cursor(), pv.cursor()
            chain = Chain(dve, self_v, NT * 11, NT * 11 + 10)
            v = nc.vector

            def rsqrt(y, yint, a, x, done):
                chain.link(v.tensor_scalar(yint, x.bitcast(I32), 1, None, ALU.arith_shift_right))
                chain.link(v.tensor_scalar(yint, yint, -1.0, float(MAGIC), ALU.mult, ALU.add))
                yf = yint.bitcast(F32)
                for i in range(3):
                    chain.link(v.scalar_tensor_tensor(out=a, in0=yf, scalar=-0.5, in1=yf, op0=ALU.mult, op1=ALU.mult))
                    chain.link(v.tensor_tensor(a, a, x, ALU.mult))
                    dst = y if i == 2 else yf
                    last = v.scalar_tensor_tensor(out=dst, in0=a, scalar=1.5, in1=yf, op0=ALU.add, op1=ALU.mult)
                    if i < 2:
                        chain.link(last)
                    else:
                        last.then_inc(done, 1)

            def step(u, j):
                A, Bm, Ck = has(u, j, 0), has(u, j, 1), has(u, j, 2)
                F_ = not (isinstance(u, int) and u == 0)
                um, jm = where(u, j, 1)
                uk, jk = where(u, j, 2)
                n, m, k = u * NT + j, um * NT + jm, uk * NT + jk
                up = F_ and j == 3
                lf = bass.ds((u - 1) // B, 1)

                def rotate(s):
                    if not A:
                        return
                    bank, q, full, free = pj.next()
                    dve.wait_ge(sq_in, 4 * n + s + 1)
                    wait(dve, qk_in, 4 * n + s - 3)
                    x3 = bank[:, :].rearrange("p (h d) -> p h d", d=DH)
                    x4 = bank[:, :].rearrange("p (h a d) -> p h a d", a=2, d=DH // 2)
                    tb = tab[:, bass.ds(u // B, 1), s % 2, :, j, :].rearrange("p o c d -> p (o c) d")
                    v.tensor_tensor(qk[:, j % 2, s, :].rearrange("p (h d) -> p h d", d=DH), x3, tb[:, 0, :].unsqueeze(1).broadcast_to([P, 8, DH]), ALU.mult)
                    v.tensor_tensor(t2[:, s, :, :].rearrange("p h (a d) -> p h a d", a=2), x4[:, :, ::-1, :],
                                    tb[:, 1, :].rearrange("p (a d) -> p a d", a=2).unsqueeze(1)
                                    .broadcast_to([P, 8, 2, DH // 2]), ALU.mult).then_inc(free, 1)
                    v.tensor_reduce(ss[:, s, :], sq[:, s % 2, :].rearrange("p (h d) -> p h d", d=DH), X, ALU.add)\
                        .then_inc(rot_in, 1)

                def norms():
                    if not A:
                        return
                    dve.wait_ge(rot_in, 4 * n + 4)
                    chain.link(v.tensor_scalar(ss[:, :, :], ss[:, :, :], 1e-24, None, ALU.max))
                    wait(dve, qk_in, 4 * (n - 1))
                    rsqrt(rn[:, j % 2, :, :], yi[:, :, :].bitcast(I32), na[:, :, :], ss[:, :, :], rn_in)

                def inverse(t, r, on):
                    if not on:
                        return
                    dve.wait_ge(ex_in, 2 * t + r + 1)
                    wait(dve, p_in, 2 * t + r - 1)
                    v.reciprocal(rr[:, 8 * r:8 * r + 8], rs[:, 8 * r:8 * r + 8]).then_inc(rr_in, 1)

                def maxima(r):
                    if not Bm:
                        return
                    w = P + W if jm > 0 else P
                    wait(dve, ex_in, 2 * (m - 1) + r + 1)
                    for e in range(2):
                        bank, q, full, free = scc.next()
                        dve.wait_ge(full, q + 1)
                        v.tensor_tensor(sm[:, 8 * r + 4 * e:8 * r + 4 * e + 4, 0:P],
                                        bank[:, :].rearrange("p (i t) -> p i t", t=P),
                                        table("band").unsqueeze(1).broadcast_to([P, 4, P]), ALU.add).then_inc(free, 1)
                        own = (free, q + 1)
                    if jm > 0:
                        bank, q, full, free = bc.next()
                        dve.wait_ge(full, q + 1)
                        v.tensor_tensor(sm[0:W, 8 * r:8 * r + 8, P:P + W],
                                        bank[0:W, 0:8 * W].rearrange("p (i t) -> p i t", t=W),
                                        table("back")[0:W, :].unsqueeze(1).broadcast_to([W, 8, W]), ALU.add)\
                            .then_inc(free, 1)
                        own = (free, q + 1)
                    dve.wait_ge(*own)
                    v.tensor_reduce(mx[:, 8 * r:8 * r + 8], sm[:, 8 * r:8 * r + 8, 0:w], X, ALU.max,
                                    negate=True).then_inc(mx_in, 1)

                def add_attention():
                    if not Ck:
                        return
                    pc.next()
                    pc.next()
                    bank, q, full, free = pc.next()
                    dve.wait_ge(full, q + 1)
                    y = yT[:, bass.ds(uk % B, 1), 1 + jk * P:1 + (jk + 1) * P].rearrange("p o t -> p (o t)")
                    v.tensor_tensor(y, bank[:, 0:P], y, ALU.add).then_inc(free, 1)

                def ffn_centre():
                    bank, q, full, free = pj.next()
                    dve.wait_ge(full, q + 1)
                    v.tensor_tensor(d2[:, :], s2[:, :], bank[:, :], ALU.subtract).then_inc(free, 1)

                def ffn_rstd():
                    bank, q, full, free = pj.next()
                    dve.wait_ge(full, q + 1)
                    v.tensor_scalar(v2[:, :], bank[:, 0:NT], EPS, None, ALU.add).then_inc(free, 1)
                    dve.wait_ge(free, q + 1)
                    rsqrt(r2[:, :], y2[:, :].bitcast(I32), a2[:, :], v2[:, :], r1_in)
                    dve.wait_ge(r1_in, u)
                    v.tensor_tensor(diag[:, :, :], ident.unsqueeze(1).broadcast_to([P, NT, P]),
                                    r2[:, :].unsqueeze(2).broadcast_to([P, NT, P]), ALU.mult).then_inc(r2_in, 1)

                def ffn_norm():
                    bank, q, full, free = pc.next()
                    dve.wait_ge(full, q + 1)
                    v.scalar_tensor_tensor(out=d2[:, :], in0=d2[:, :], scalar=vecs[:, 0, lf], in1=bank[:, :],
                                           op0=ALU.mult, op1=ALU.mult).then_inc(free, 1)
                    dve.wait_ge(free, q + 1)
                    v.memset(tiny[:, B:B + 1], 0.0).then_inc(xg_in, 1)

                def ffn_gate(i):
                    lo, w = FCH[i]
                    _, q, _, free = pj.next()
                    dve.wait_ge(free, q + 1)
                    bank, q, full, free = pj.next()
                    dve.wait_ge(full, q + 1)
                    v.scalar_tensor_tensor(out=ag[i][0:w], in0=bank[0:w, :],
                                           scalar=b1[0:w, lf, 0, i:i + 1].rearrange("p a b -> p (a b)"),
                                           in1=gg[0:w, i % 2, :], op0=ALU.add, op1=ALU.mult).then_inc(free, 1)

                def ffn_add():
                    bank, q, full, free = pc.next()
                    dve.wait_ge(full, q + 1)
                    y = yT[:, bass.ds((u - 1) % B, 1), 1:S + 1].rearrange("p o t -> p (o t)")
                    v.scalar_tensor_tensor(out=y, in0=bank[:, :], scalar=vecs[:, 2, lf], in1=y,
                                           op0=ALU.add, op1=ALU.add).then_inc(free, 1)
                    dve.wait_ge(free, q + 1)
                    v.memset(tiny[:, B + 1:B + 2], 0.0).then_inc(f_done, 1)

                rotate(0)
                rotate(1)
                inverse(k, 1, Ck)
                rotate(2)
                maxima(0)
                if Ck and jk > 0:
                    bc.next()
                rotate(3)
                if up:
                    ffn_norm()
                norms()
                if A:
                    pj.next()
                if F_ and j == 2:
                    ffn_centre()
                if A:
                    pj.next()
                maxima(1)
                if Ck and jk > 0:
                    bc.next()
                inverse(m, 0, Bm)
                if up:
                    ffn_gate(0)
                    ffn_gate(1)
                if F_ and j == 2:
                    ffn_rstd()
                if up:
                    ffn_gate(2)
                add_attention()
                if up:
                    ffn_add()

            for b in range(B):
                v.memset(tiny[:, b:b + 1], 0.0).then_inc(f_done, 1)
            it = steps((pj, scc, bc, pc, chain), step)
            it(0)
            with dve.Fori(1, UNITS) as u:
                it(u)
            it(UNITS, check=False)
            dve.wait_ge(f_done, B + UNITS)
            for b in range(B):
                v.tensor_tensor(xT[:, b, :], yT[:, b, 1:S + 1], xT[:, b, :], ALU.add)

        @block.gpsimd
        def _(pool):
            chain = Chain(pool, self_p, 4 * NT, 4 * NT)
            g = nc.gpsimd

            def shifted(dst, b, at, width, done, before):
                hc = P // 2
                src = yT[:, bass.ds(b, 1), :].rearrange("p o t -> p (o t)") if not isinstance(b, int) else yT[:, b, :]
                g.tensor_copy(dst[0:hc, :], src[0:hc, at + 1:at + 1 + width]).then_inc(done, 1)
                pool.wait_ge(done, 2 * before + 1)
                g.tensor_copy(dst[hc:P, :], src[hc:P, at:at + width]).then_inc(done, 1)
                pool.wait_ge(done, 2 * before + 2)

            def step(u, j):
                A, Bm, Ck = has(u, j, 0), has(u, j, 1), has(u, j, 2)
                F_ = not (isinstance(u, int) and u == 0)
                um, jm = where(u, j, 1)
                uk, jk = where(u, j, 2)
                n, m, k = u * NT + j, um * NT + jm, uk * NT + jk

                def join(s):
                    if not A:
                        return
                    pool.wait_ge(rot_in, 4 * n + s + 1)
                    x = qk[:, j % 2, s, :].rearrange("p (h d) -> p h d", d=DH)
                    chain.link(g.tensor_tensor(x, x, t2[:, s, :, :], ALU.add))

                def normalise(s):
                    if not A:
                        return
                    pool.wait_ge(rn_in, n + 1)
                    x = qk[:, j % 2, s, :].rearrange("p (h d) -> p h d", d=DH)
                    g.tensor_tensor(x, x, rn[:, j % 2, s, :].unsqueeze(2).broadcast_to([P, 8, DH]), ALU.mult)\
                        .then_inc(qk_in, 1)

                def next_input():
                    if not A:
                        return
                    un, jn = (u, j + 1) if j < NT - 1 else (u + 1, 0)
                    pool.wait_ge(sq_in, 4 * n + 1)
                    if jn == 0:
                        pool.wait_ge(f_done, un + 1)
                    shifted(xs[:, jn % 2, :], un % B, jn * P, P, xs_in, n + 1)

                def probabilities(t, jt, r, on):
                    if not on:
                        return
                    w = P + W if jt > 0 else P
                    pool.wait_ge(rr_in, 2 * t + r + 1)
                    e = ex[:, jt % 2, 8 * r:8 * r + 8, 0:w]
                    g.tensor_tensor(e, e, rr[:, 8 * r:8 * r + 8].unsqueeze(2).broadcast_to([P, 8, w]), ALU.mult)\
                        .then_inc(p_in, 1)

                join(0)
                join(1)
                probabilities(k, jk, 1, Ck)
                if F_ and j == 2:
                    pool.wait_ge(pv.free[0], pv_before(u) + 6)
                    shifted(s2[:, :], (u - 1) % B, 0, S, s2_in, u - 1)
                next_input()
                join(2)
                join(3)
                for s in range(4):
                    normalise(s)
                probabilities(m, jm, 0, Bm)

            pool.wait_ge(f_done, 1)
            shifted(xs[:, 0, :], 0, 0, P, xs_in, 0)
            it = steps((chain,), step)
            it(0)
            with pool.Fori(1, UNITS) as u:
                it(u)
            it(UNITS, check=False)


def net(nc, ins, out, consts, place, phases="ABCD"):
    ctx = ExitStack()
    with ctx:
        def sb(name, shape, c=ctx, dt=F32):
            return c.enter_context(nc.sbuf_tensor(name, shape, dt))

        def sem(name, c=ctx):
            return c.enter_context(nc.semaphore(name))

        xT = sb("xT", [P, B, S])
        yT = sb("yT", [P, B, S + 1])
        cst = sb("cst", [P, consts.shape[1]])
        ones = sb("ones", [P, P])
        mean_w = sb("mean_w", [P, P])
        eps = sb("eps", [P, 1])
        ctxT = sb("ctxT", [P, B, SK])
        psum = [ctx.enter_context(nc.psum_tensor(f"bank{i}", [P, 512], F32)) for i in range(8)]

        def table(name):
            at, n = place[name]
            return cst[:, at:at + n]

        ident = table("ident")

        layernorm_count = [0]

        def layernorm(src, dst):
            n = layernorm_count[0]
            layernorm_count[0] += 1
            with ExitStack() as c:
                d = sb(f"ln_d{n}", [P, B, S], c)
                sq = sb(f"ln_sq{n}", [P, B, S], c)
                sd = sb(f"ln_sd{n}", [P, B, S], c)
                rs = sb(f"ln_rs{n}", [P, B, S], c)
                mean_done, d_done = sem(f"mean_done{n}", c), sem(f"d_done{n}", c)
                sq_done, var_done = sem(f"sq_done{n}", c), sem(f"var_done{n}", c)
                sd_done, rs_done = sem(f"sd_done{n}", c), sem(f"rs_done{n}", c)
                block = c.enter_context(nc.Block())

                @block.tensor
                def _(pe):
                    for b in range(B):
                        nc.tensor.matmul(psum[b][:, :], mean_w[:, :], src(b), start=True, stop=True)\
                            .then_inc(mean_done, 1)
                    for b in range(B):
                        pe.wait_ge(sq_done, b + 1)
                        nc.tensor.matmul(psum[4 + b][:, :], mean_w[:, :], sq[:, b, :], start=True, stop=True)\
                            .then_inc(var_done, 1)

                @block.scalar
                def _(act):
                    for b in range(B):
                        act.wait_ge(d_done, b + 1)
                        nc.scalar.activation(sq[:, b, :], d[:, b, :], ACT.Square).then_inc(sq_done, 1)
                    for b in range(B):
                        act.wait_ge(var_done, b + 1)
                        nc.scalar.activation(sd[:, b, :], psum[4 + b][:, :], ACT.Sqrt, bias=eps[:, 0:1])\
                            .then_inc(sd_done, 1)

                @block.vector
                def _(dve):
                    for b in range(B):
                        dve.wait_ge(mean_done, b + 1)
                        nc.vector.tensor_tensor(d[:, b, :], src(b), psum[b][:, :], ALU.subtract)\
                            .then_inc(d_done, 1)
                    for b in range(B):
                        dve.wait_ge(sd_done, b + 1)
                        nc.vector.reciprocal(rs[:, b, :], sd[:, b, :]).then_inc(rs_done, 1)
                    for b in range(B):
                        dve.wait_ge(rs_done, b + 1)
                        nc.vector.tensor_tensor(dst(b), d[:, b, :], rs[:, b, :], ALU.mult)

        with ExitStack() as c:
            xtok = sb("xtok", [P, B * NT, P], c)
            ctok = sb("ctok", [SK, B, P], c)
            x_in, c_in, k_in = sem("x_in", c), sem("c_in", c), sem("k_in", c)
            xt_full, xt_done = sem("xt_full", c), sem("xt_done", c)
            block = c.enter_context(nc.Block())

            @block.sync
            def _(sp):
                sp.dma_start(cst[:, :], consts).then_inc(k_in, 16)
                sp.dma_start(xtok[:, :, :], ins["x"].rearrange("b (t p) d -> p (b t) d", p=P)).then_inc(x_in, 16)
                sp.dma_start(ctok[:, :, :], ins["ctx_1024"].rearrange("b s d -> s b d")).then_inc(c_in, 16)

            @block.vector
            def _(dve):
                nc.vector.memset(ones[:, :], 1.0)
                nc.vector.memset(mean_w[:, :], 1.0 / P)
                nc.vector.memset(eps[:, :], EPS)
                nc.vector.memset(yT[:, :, 0:1], 0.0)

            @block.tensor
            def _(pe):
                pe.wait_ge(k_in, 16)
                pe.wait_ge(x_in, 16)
                for b in range(B):
                    for t in range(NT):
                        last = nc.tensor.transpose(psum[b][:, t * P:(t + 1) * P], xtok[:, b * NT + t, :], ident)
                    last.then_inc(xt_full, 1)
                pe.wait_ge(c_in, 16)
                for b in range(B):
                    last = nc.tensor.transpose(psum[4][:, b * SK:(b + 1) * SK], ctok[:, b, :], ident[0:SK, 0:SK])
                last.then_inc(xt_full, 1)

            @block.scalar
            def _(act):
                for b in range(B):
                    act.wait_ge(xt_full, b + 1)
                    nc.scalar.activation(xT[:, b, :], psum[b][:, :], ACT.Copy)
                act.wait_ge(xt_full, B + 1)
                nc.scalar.activation(ctxT[:, :, :], psum[4][:, 0:B * SK].rearrange("p (b s) -> p b s", s=SK), ACT.Copy)

        def x_of(b):
            return xT[:, b, :]

        def y_of(b):
            return yT[:, b, 1:S + 1]

        def cross(kind):
            first = kind == "A"
            scale = 8.0 ** -0.5 if first else 64.0 ** -0.5
            with ExitStack() as c:
                def s_(n):
                    return sem(f"{kind}_{n}", c)

                def b_(n, shape, dt=F32):
                    return sb(f"{kind}_{n}", shape, c, dt)

                w_in = s_("w_in")
                wt_full, wt_done = s_("wt_full"), s_("wt_done")
                kv_full, kv_done = s_("kv_full"), s_("kv_done")
                kT, vT = b_("kT", [P, B, SK]), b_("vT", [P, B, SK])
                if first:
                    wq, wk, wv, wo = (b_(n, [P, P]) for n in ("wq", "wk", "wv", "wo"))
                    bias = b_("bias", [P, 4])
                    wkT, wvT, woT = (b_(n, [P, P]) for n in ("wkT", "wvT", "woT"))
                    bq_rep = b_("bq_rep", [P, P])
                    wo_heads = b_("wo_heads", [P, H, P])
                    mask8 = b_("mask8", [P, B, SK], mybir.dt.uint8)
                    maskf = b_("maskf", [P, B, SK])
                    kv, vv = b_("kv", [P, H, SK]), b_("vv", [P, SK])
                    mask_b = b_("mask_b", [P, H, SK])
                else:
                    wq, wqT = b_("wq", [P, H * DH]), b_("wqT", [P, 8, P])
                    wk2, wv2 = b_("wk2", [P, 2, DH]), b_("wv2", [P, 2, DH])
                    wo = b_("wo", [P, 8, P])
                    kv, vv = b_("kv", [P, 2, SK]), b_("vv", [P, 2, SK])
                G = b_("G", [P, H, SK])
                U = b_("U", [SK, H, P])
                xs = b_("xs", [P, 2, P])
                sm = b_("sm", [P, 2, H, SK])
                ex = b_("ex", [P, 2, H, SK])
                mx, den, rden = b_("mx", [P, 2, H]), b_("den", [P, H]), b_("rden", [P, 2, H])
                pT = b_("pT", [SK, 2, H, P])

                kv_in = s_("kv_in")
                mask_in = s_("mask_in")
                xs_in = s_("xs_in")
                sc_full, sc_done = s_("sc_full"), s_("sc_done")
                mx_done, sub_done = s_("mx_done"), s_("sub_done")
                ex_done, rd_done = s_("ex_done"), s_("rd_done")
                p_done = s_("p_done")
                o_full, o_done = s_("o_full"), s_("o_done")
                self_v = s_("self_v")
                GJ = HJ if first else [(0, 4), (4, 4), (8, 4), (12, 4)]
                NPREP = len(GJ) + 4 + (len(HJ) if first else 0)
                prep = Ring(c, nc, f"{kind}_prep", [psum[5], psum[6]], NPREP, NPREP)
                pt = Ring(c, nc, f"{kind}_pt", [psum[3], psum[4]], 16, 16)

                c1 = ExitStack()
                block = c1.enter_context(nc.Block())

                @block.sync
                def _(sp):
                    if first:
                        for t, n in ((wq, "w_q"), (wk, "w_k"), (wv, "w_v"), (wo, "w_o")):
                            sp.dma_start(t[:, :], ins["L0_xattn_" + n]).then_inc(w_in, 16)
                        for i, n in enumerate(("b_q", "b_k", "b_v", "b_o")):
                            sp.dma_start(bias[:, i:i + 1], ins["L0_xattn_" + n].rearrange("(p o) -> p o", o=1))\
                                .then_inc(w_in, 16)
                        m = ins["mask_Bx1x1xS2_bf1"].rearrange("b i j s -> (i j) b s").broadcast_to([P, B, SK])
                        sp.dma_start(mask8[:, :, :], m).then_inc(w_in, 16)
                    else:
                        sp.dma_start(wq[:, :], ins["L1_xattn_W_q"]).then_inc(w_in, 16)
                        for a in range(2):
                            sp.dma_start(wk2[:, a, :], ins["L1_xattn_W_k"]).then_inc(w_in, 16)
                            sp.dma_start(wv2[:, a, :], ins["L1_xattn_W_v"]).then_inc(w_in, 16)
                        sp.dma_start(wo[:, :, :], ins["L1_xattn_W_o"].rearrange("(c p) o -> p c o", p=P))\
                            .then_inc(w_in, 16)

                @block.tensor
                def _(pe):
                    pe.wait_ge(w_in, 16 * (9 if first else 6))
                    if first:
                        for i, t in enumerate((wk, wv, wo)):
                            last = nc.tensor.transpose(psum[0][:, i * P:(i + 1) * P], t[:, :], ident)
                        last.then_inc(wt_full, 1)
                    else:
                        for g in range(2):
                            for i in range(4):
                                cc = 4 * g + i
                                last = nc.tensor.transpose(psum[g][:, i * P:(i + 1) * P],
                                                           wq[:, cc * P:(cc + 1) * P], ident)
                            last.then_inc(wt_full, 1)
                    pe.wait_ge(wt_done, 1)
                    lk = wkT[:, :] if first else wk2[:, :, :].rearrange("p a d -> p (a d)")
                    lv = wvT[:, :] if first else wv2[:, :, :].rearrange("p a d -> p (a d)")
                    for i, lhs in enumerate((lk, lv)):
                        nc.tensor.matmul(psum[2 + i][:, 0:B * SK], lhs, ctxT[:, :, :].rearrange("p b s -> p (b s)"),
                                         start=True, stop=True).then_inc(kv_full, 1)

                @block.scalar
                def _(act):
                    if first:
                        act.wait_ge(wt_full, 1)
                        nc.scalar.activation(wkT[:, :], psum[0][:, 0:P], ACT.Copy)
                        nc.scalar.activation(wvT[:, :], psum[0][:, P:2 * P], ACT.Copy)
                        nc.scalar.activation(woT[:, :], psum[0][:, 2 * P:3 * P], ACT.Copy).then_inc(wt_done, 1)
                    else:
                        for g in range(2):
                            act.wait_ge(wt_full, g + 1)
                            last = nc.scalar.activation(wqT[:, 4 * g:4 * g + 4, :].rearrange("p c i -> p (c i)"),
                                                        psum[g][:, :], ACT.Copy)
                        last.then_inc(wt_done, 1)
                    for i, t in enumerate((kT, vT)):
                        act.wait_ge(kv_full, i + 1)
                        src = psum[2 + i][:, 0:B * SK].rearrange("p (b s) -> p b s", s=SK)
                        if first:
                            nc.scalar.activation(t[:, :, :], src, ACT.Identity, bias=bias[:, 1 + i:2 + i])
                        else:
                            nc.scalar.activation(t[:, :, :], src, ACT.Copy)

                @block.vector
                def _(dve):
                    if first:
                        dve.wait_ge(w_in, 16 * 9)
                        nc.vector.tensor_scalar(maskf[:, :, :], mask8[:, :, :], -NEG, NEG, ALU.mult, ALU.add)
                        nc.vector.tensor_scalar(bq_rep[:, :], ones[:, :], bias[:, 0:1], None, ALU.mult)
                        dve.wait_ge(wt_done, 1)
                        nc.vector.tensor_tensor(wo_heads[:, :, :], woT[:, :].unsqueeze(1).broadcast_to([P, H, P]),
                                                table("heads8").unsqueeze(2).broadcast_to([P, H, P]), ALU.mult)

                c1.close()
                block = c.enter_context(nc.Block())

                @block.tensor
                def _(pe):
                    prep_c, pt_c = prep.cursor(), pt.cursor()

                    def fill(g):
                        bank, q, full, free = prep_c.next()
                        wait(pe, free, q)
                        g(bank).then_inc(full, 1)
                        return free, q + 1

                    def a_product(bank, lhs, rhs):
                        return nc.tensor.matmul(bank[0:lhs.shape[-1], 0:rhs.shape[-1]], lhs, rhs, start=True, stop=True)

                    def g_of_pairs(bank, h0):
                        for i in range(2):
                            last = nc.tensor.matmul(bank[:, 2 * i * SK:2 * (i + 1) * SK], wqT[:, h0 // 2 + i, :],
                                                    kv[:, :, :].rearrange("p a s -> p (a s)"), start=True, stop=True)
                        return last

                    def u_of_heads(bank, h0):
                        for i in range(4):
                            h = h0 + i
                            last = nc.tensor.matmul(bank[0:SK, i * P:(i + 1) * P], vv[:, h % 2, :], wo[:, h // 2, :],
                                                    start=True, stop=True)
                        return last

                    def body(b):
                        prep_c.begin(b)
                        pt_c.begin(b)
                        pe.wait_ge(kv_in, b + 1)
                        if first:
                            heads = [kv[:, h0:h0 + nh, :].rearrange("p h s -> p (h s)") for h0, nh in HJ]
                            for k in heads:
                                fill(lambda t: a_product(t, wq[:, :], k))
                            for k in heads:
                                fill(lambda t: a_product(t, bq_rep[:, :], k))
                            for g in range(4):
                                rhs = wo_heads[:, 4 * g:4 * g + 4, :].rearrange("p h o -> p (h o)")
                                done = [*(done[-1:] if g else []), fill(lambda t: a_product(t, vv[:, :], rhs))]
                        else:
                            for g in range(4):
                                fill(lambda t: g_of_pairs(t, 4 * g))
                            for g in range(4):
                                done = [*(done[-1:] if g else []), fill(lambda t: u_of_heads(t, 4 * g))]
                        for free, q in done:
                            pe.wait_ge(free, q)

                        def scores(j):
                            t = b * NT + j
                            pe.wait_ge(xs_in, t + 1)
                            wait(pe, sc_done, t * 3)
                            for k, (h0, nh) in enumerate(HJ):
                                nc.tensor.matmul(psum[k][:, 0:nh * SK], xs[:, j % 2, :],
                                                 G[:, h0:h0 + nh, :].rearrange("p h s -> p (h s)"),
                                                 start=True, stop=True).then_inc(sc_full, 1)

                        def outputs(j):
                            t = b * NT + j
                            pe.wait_ge(p_done, t + 1)
                            moved = []
                            for g in range(4):
                                bank, q, full, free = pt_c.next()
                                wait(pe, free, q)
                                for i in range(4):
                                    last = nc.tensor.transpose(bank[0:SK, i * P:(i + 1) * P],
                                                               ex[:, j % 2, 4 * g + i, :], ident)
                                last.then_inc(full, 1)
                                moved = moved[-1:] + [(free, q + 1)]
                            for free, q in moved:
                                pe.wait_ge(free, q)
                            wait(pe, o_done, t)
                            for h in range(H):
                                last = nc.tensor.matmul(psum[7][:, 0:P], U[:, h, :], pT[:, j % 2, h, :],
                                                        start=(h == 0), stop=(h == H - 1))
                            last.then_inc(o_full, 1)

                        scores(0)
                        for j in range(1, NT):
                            scores(j)
                            outputs(j - 1)
                        outputs(NT - 1)
                        prep_c.end()
                        pt_c.end()

                    body(0)
                    with pe.Fori(1, B) as b:
                        body(b)

                @block.scalar
                def _(act):
                    prep_c, pt_c = prep.cursor(), pt.cursor()

                    def take(dst, width, rows=P, scale=1.0):
                        bank, q, full, free = prep_c.next()
                        act.wait_ge(full, q + 1)
                        nc.scalar.activation(dst, bank[0:rows, 0:width], ACT.Copy, scale=scale).then_inc(free, 1)

                    def body(b):
                        prep_c.begin(b)
                        pt_c.begin(b)
                        wait(act, o_done, b * NT)
                        for h0, nh in GJ:
                            take(G[:, h0:h0 + nh, :].rearrange("p h s -> p (h s)"), nh * SK)
                        if first:
                            for h0, nh in HJ:
                                take(mask_b[:, h0:h0 + nh, :].rearrange("p h s -> p (h s)"), nh * SK, scale=scale)
                        for g in range(4):
                            take(U[:, 4 * g:4 * g + 4, :].rearrange("p h o -> p (h o)"), 4 * P, rows=SK)

                        def exponentials(j):
                            act.wait_ge(sub_done, b * NT + j + 1)
                            e = ex[:, j % 2, :, :].rearrange("p h s -> p (h s)")
                            nc.scalar.activation(e, e, ACT.Exp).then_inc(ex_done, 1)

                        def copies(j):
                            wait(act, o_done, b * NT + j - 1)
                            for g in range(4):
                                bank, q, full, free = pt_c.next()
                                act.wait_ge(full, q + 1)
                                nc.scalar.activation(pT[:, j % 2, 4 * g:4 * g + 4, :].rearrange("p h o -> p (h o)"),
                                                     bank[0:SK, :], ACT.Copy).then_inc(free, 1)

                        exponentials(0)
                        for j in range(1, NT):
                            exponentials(j)
                            copies(j - 1)
                        copies(NT - 1)
                        prep_c.end()
                        pt_c.end()

                    body(0)
                    with act.Fori(1, B) as b:
                        body(b)

                @block.vector
                def _(dve):
                    chain = Chain(dve, self_v, NT + first, NT + first)
                    prep_c = prep.cursor()

                    def body(b):
                        chain.begin(b)
                        prep_c.begin(b)
                        wait(dve, o_done, b * NT)
                        if first:
                            nc.vector.tensor_tensor(kv[:, :, :], kT[:, b, :].unsqueeze(1).broadcast_to([P, H, SK]),
                                                    table("heads8").unsqueeze(2).broadcast_to([P, H, SK]), ALU.mult)
                            nc.vector.tensor_copy(vv[:, :], vT[:, b, :]).then_inc(kv_in, 1)
                            for _ in range(6):
                                bank, q, full, free = prep_c.next()
                                last_two = (free, q + 1)
                                if _ >= 4:
                                    dve.wait_ge(free, q + 1)
                            chain.link(nc.vector.tensor_tensor(
                                mask_b[:, :, :], mask_b[:, :, :],
                                maskf[:, b, :].unsqueeze(1).broadcast_to([P, H, SK]), ALU.add))
                        else:
                            for t, s in ((kv, kT), (vv, vT)):
                                last = nc.vector.tensor_tensor(
                                    t[:, :, :], s[:, b, :].unsqueeze(1).broadcast_to([P, 2, SK]),
                                    table("halves").unsqueeze(2).broadcast_to([P, 2, SK]), ALU.mult)
                            last.then_inc(kv_in, 1)

                        def maxima(j):
                            t = b * NT + j
                            for k, (h0, nh) in enumerate(HJ):
                                dve.wait_ge(sc_full, 3 * t + k + 1)
                                if first:
                                    m = mask_b[:, h0:h0 + nh, :]
                                else:
                                    m = table("causal")[:, j * SK:(j + 1) * SK].unsqueeze(1).broadcast_to([P, nh, SK])
                                nc.vector.scalar_tensor_tensor(
                                    out=sm[:, j % 2, h0:h0 + nh, :],
                                    in0=psum[k][:, 0:nh * SK].rearrange("p (h s) -> p h s", s=SK),
                                    scalar=scale, in1=m, op0=ALU.mult, op1=ALU.add).then_inc(sc_done, 1)
                            dve.wait_ge(sc_done, 3 * t + 3)
                            nc.vector.tensor_reduce(mx[:, j % 2, :], sm[:, j % 2, :, :], X, ALU.max).then_inc(mx_done, 1)

                        def sums(j):
                            dve.wait_ge(ex_done, b * NT + j + 1)
                            wait(dve, p_done, b * NT + j - 1)
                            chain.link(nc.vector.tensor_reduce(den[:, :], ex[:, j % 2, :, :], X, ALU.add))
                            nc.vector.reciprocal(rden[:, j % 2, :], den[:, :]).then_inc(rd_done, 1)

                        def add(j):
                            t = b * NT + j
                            dve.wait_ge(o_full, t + 1)
                            xt = xT[:, b, j * P:(j + 1) * P]
                            if first:
                                nc.vector.scalar_tensor_tensor(out=xt, in0=psum[7][:, 0:P], scalar=bias[:, 3:4], in1=xt,
                                                               op0=ALU.add, op1=ALU.add).then_inc(o_done, 1)
                            else:
                                nc.vector.tensor_tensor(xt, psum[7][:, 0:P], xt, ALU.add).then_inc(o_done, 1)

                        maxima(0)
                        for j in range(1, NT):
                            maxima(j)
                            sums(j - 1)
                            if j >= 2:
                                add(j - 2)
                        sums(NT - 1)
                        add(NT - 2)
                        add(NT - 1)
                        chain.end()

                    body(0)
                    with dve.Fori(1, B) as b:
                        body(b)

                @block.gpsimd
                def _(pool):
                    def body(b):
                        def inputs(j):
                            t = b * NT + j
                            wait(pool, sc_done, 3 * t - 3)
                            nc.gpsimd.tensor_copy(xs[:, j % 2, :], yT[:, b, 1 + j * P:1 + (j + 1) * P]).then_inc(xs_in, 1)

                        def subtract(j):
                            t = b * NT + j
                            pool.wait_ge(mx_done, t + 1)
                            wait(pool, o_done, t - 1)
                            nc.gpsimd.tensor_tensor(ex[:, j % 2, :, :], sm[:, j % 2, :, :],
                                                    mx[:, j % 2, :].unsqueeze(2).broadcast_to([P, H, SK]),
                                                    ALU.subtract).then_inc(sub_done, 1)

                        def normalise(j):
                            pool.wait_ge(rd_done, b * NT + j + 1)
                            nc.gpsimd.tensor_tensor(ex[:, j % 2, :, :], ex[:, j % 2, :, :],
                                                    rden[:, j % 2, :].unsqueeze(2).broadcast_to([P, H, SK]),
                                                    ALU.mult).then_inc(p_done, 1)

                        inputs(0)
                        inputs(1)
                        subtract(0)
                        for j in range(1, NT):
                            subtract(j)
                            normalise(j - 1)
                            if j + 1 < NT:
                                inputs(j + 1)
                        normalise(NT - 1)

                    body(0)
                    with pool.Fori(1, B) as b:
                        body(b)

        if "A" in phases:
            layernorm(x_of, y_of)
            cross("A")
        if "B" in phases:
            layernorm(x_of, y_of)
            local(nc, ctx, locals())
        if "C" in phases:
            layernorm(x_of, y_of)
            cross("C")
        if "D" in phases:
            layernorm(x_of, y_of)
            experts(nc, ctx, locals())

        with ExitStack() as c:
            otok = sb("otok", [P, B * NT, P], c)
            xt_full, out_in, stored = sem("ot_full", c), sem("out_in", c), sem("stored", c)
            block = c.enter_context(nc.Block())

            @block.tensor
            def _(pe):
                for b in range(B):
                    for t in range(NT):
                        last = nc.tensor.transpose(psum[b][:, t * P:(t + 1) * P], xT[:, b, t * P:(t + 1) * P], ident)
                    last.then_inc(xt_full, 1)

            @block.vector
            def _(dve):
                for b in range(B):
                    dve.wait_ge(xt_full, b + 1)
                    nc.vector.tensor_copy(otok[:, b * NT:(b + 1) * NT, :].rearrange("p t d -> p (t d)"), psum[b][:, :])\
                        .then_inc(out_in, 1)

            @block.sync
            def _(sp):
                for b in range(B):
                    sp.wait_ge(out_in, b + 1)
                    sp.dma_start(out[b, :, :].rearrange("(t p) d -> p t d", p=P), otok[:, b * NT:(b + 1) * NT, :])\
                        .then_inc(stored, 16)
                sp.wait_ge(stored, 16 * B)


NAMES = ["x", "ctx_1024", "mask_Bx1x1xS2_bf1", "L0_xattn_w_q", "L0_xattn_b_q", "L0_xattn_w_k", "L0_xattn_b_k",
         "L0_xattn_w_v", "L0_xattn_b_v", "L0_xattn_w_o", "L0_xattn_b_o", "L0_ffn_Wqkv", "L0_ffn_q_scale",
         "L0_ffn_k_scale", "L0_ffn_Wo", "L0_ffn_ln_g", "L0_ffn_ln_b", "L0_ffn_W1", "L0_ffn_b1", "L0_ffn_W2",
         "L0_ffn_b2", "L1_xattn_W_q", "L1_xattn_W_k", "L1_xattn_W_v", "L1_xattn_W_o", "L1_ffn_Wg", "L1_ffn_bg",
         "L1_ffn_W1", "L1_ffn_b1", "L1_ffn_W2", "L1_ffn_b2"]


def kernel(**inputs):
    import concourse.bacc as bacc
    from concourse.bass_utils import run_bass_kernel_spmd

    nc = bacc.Bacc("TRN2", target_bir_lowering=False, num_devices=1)
    arrays, aps = {}, {}
    for name in NAMES:
        a = np.ascontiguousarray(inputs[name])
        if a.dtype == np.bool_:
            a = a.view(np.uint8)
        if name in ("L0_ffn_ln_g", "L0_ffn_ln_b", "L0_ffn_b2"):
            a = np.ascontiguousarray(a.T)
        if name == "L0_ffn_b1":
            a = np.pad(a.reshape(DEPTH, 2, FI), ((0, 0), (0, 0), (0, 3 * P - FI)))
            a = np.ascontiguousarray(a.reshape(DEPTH, 2, 3, P).transpose(3, 0, 1, 2))
        if name == "L1_ffn_b1":
            a = np.ascontiguousarray(a.reshape(E, FF // P, P).transpose(2, 0, 1))
        arrays[name] = a
        aps[name] = nc.dram_tensor(name, a.shape, mybir.dt.from_np(a.dtype), kind="ExternalInput").ap()
    consts, place = constants()
    arrays["shape_tables"] = consts
    tables = nc.dram_tensor("shape_tables", consts.shape, F32, kind="ExternalInput").ap()
    out = nc.dram_tensor("out", (B, S, P), F32, kind="ExternalOutput").ap()
    net(nc, aps, out, tables, place)
    r = run_bass_kernel_spmd(nc, [arrays], core_ids=[0])
    return r.results[0]["out"]
```

```python
from contextlib import ExitStack

import concourse.bass as bass
from concourse import mybir
import numpy as np

F32 = mybir.dt.float32
I32 = mybir.dt.int32
ALU = mybir.AluOpType
ACT = mybir.ActivationFunctionType
X = mybir.AxisListType.X

P = 128
B, S = 4, 512
NT = S // P
H = 16
SK = 77
DEPTH = 6
DH = 64
W = 32
FI = 341
FCH = [(0, 128), (128, 128), (256, FI - 256)]
UNITS = DEPTH * B
E, R, FF = 4, 4, 512
NEG = -3.0e38
EPS = 1e-5
HJ = [(0, 6), (6, 6), (12, 4)]
MAGIC = 0x5F3759DF


def constants():
    f = np.float32
    half = np.arange(0, DH, 2, dtype=f)
    inv_freq = (f(1.0) / np.power(f(10000.0), half / f(DH))).astype(f)
    t = np.arange(S, dtype=f)
    freqs = t[:, None] * inv_freq[None, :]
    freqs = np.concatenate([freqs, freqs], -1)
    base = ((half + f(0.4 * DH)) / f(1.4 * DH)).astype(f)
    scale = np.power(base[None, :], ((t - S // 2) / f(W // 2))[:, None]).astype(f)
    scale = np.concatenate([scale, scale], -1)
    sign = np.where(np.arange(DH) < DH // 2, -1.0, 1.0).astype(f)
    cos, sin = np.cos(freqs), np.sin(freqs) * sign
    rot = np.zeros((P, 2, 2, NT, DH), f)
    for qk, m in enumerate((scale * f(8.0), f(1.0) / scale)):
        for cs, w in enumerate((cos, sin)):
            rot[:, qk, cs] = (w * m).reshape(NT, P, DH).transpose(1, 0, 2)
    q, k = np.arange(P)[:, None], np.arange(P)[None, :]
    band = np.where((k <= q) & (q - k <= W), 0.0, NEG).astype(f)
    back = np.zeros((P, W), f)
    back[:W] = np.where(np.arange(W)[None, :] >= np.arange(W)[:, None], 0.0, NEG)
    tok = np.arange(S).reshape(NT, P).T
    causal = np.where(tok[:, :, None] >= np.arange(SK), 0.0, NEG).astype(f)
    heads8 = (np.arange(P)[:, None] // 8 == np.arange(H)[None]).astype(f)
    halves = (np.arange(P)[:, None] // DH == np.arange(2)[None]).astype(f)
    before = np.broadcast_to((np.arange(E)[None, :] < np.arange(E)[:, None]), (P, E, E)).astype(f)
    parts = dict(ident=np.eye(P, dtype=f), rot=rot, band=band, back=back, causal=causal,
                 heads8=heads8, halves=halves, before=before)
    place, at = {}, 0
    for n, a in parts.items():
        place[n] = (at, a.size // P)
        at += a.size // P
    return np.concatenate([a.reshape(P, -1) for a in parts.values()], 1), place


class Ring:

    def __init__(self, ctx, nc, name, banks, first, steady):
        self.banks = banks
        n = len(banks)
        assert first % n == 0 and steady % n == 0
        self.first, self.steady = first, steady
        self.full = [ctx.enter_context(nc.semaphore(f"{name}_full{i}")) for i in range(n)]
        self.free = [ctx.enter_context(nc.semaphore(f"{name}_free{i}")) for i in range(n)]

    def cursor(self):
        return Cursor(self)


class Cursor:
    def __init__(self, ring):
        self.ring, self.n, self.i = ring, 0, 0

    def begin(self, i):
        self.i, self.n = i, 0

    def end(self):
        first = isinstance(self.i, int) and self.i == 0
        assert self.n == (self.ring.first if first else self.ring.steady), (self.n, first)

    def next(self):
        r = self.ring
        nb = len(r.banks)
        k = self.n % nb
        q = self.n // nb
        if not (isinstance(self.i, int) and self.i == 0):
            q = self.i * (r.steady // nb) + (r.first // nb - r.steady // nb + q)
        self.n += 1
        return r.banks[k], q, r.full[k], r.free[k]


class Chain:

    def __init__(self, eng, sem, first, steady):
        self.eng, self.sem, self.first, self.steady, self.n, self.base = eng, sem, first, steady, 0, 0

    def begin(self, i):
        self.n = 0
        self.base = 0 if isinstance(i, int) and i == 0 else i * self.steady + (self.first - self.steady)

    def end(self):
        want = self.first if isinstance(self.base, int) and self.base == 0 else self.steady
        assert self.n == want, (self.n, want)

    def link(self, ins):
        self.n += 1
        ins.then_inc(self.sem, 1)
        self.eng.wait_ge(self.sem, self.base + self.n)


def wait(eng, sem, value):
    if isinstance(value, int) and value <= 0:
        return
    eng.wait_ge(sem, value)


def experts(nc, ctx, o):
    sb, sem, ins, psum, xT, yT, ident, table = (o[k] for k in ("sb", "sem", "ins", "psum", "xT", "yT", "ident", "table"))
    FC = FF // P
    with ExitStack() as c:
        w1 = sb("moe_w1", [P, E, FF], c)
        w2 = sb("moe_w2", [P, E, FC, P], c)
        b1 = sb("moe_b1", [P, E, FC], c)
        b2 = sb("moe_b2", [E, P], c)
        wg = sb("moe_wg", [P, R, E], c)
        bg = sb("moe_bg", [P, R, E], c)
        hm = sb("moe_hidden", [P, 2, FC, S], c)
        lg, sl, z, sel, cw = (sb(f"moe_{n}", [P, NT, E], c) for n in ("logits", "chosen_logits", "z", "chosen", "weights"))
        th = sb("moe_tanh", [P, NT, E], c)
        gt, ge = sb("moe_gt", [P, NT, E, E], c), sb("moe_ge", [P, NT, E, E], c)
        rank, tot = sb("moe_rank", [P, NT, E], c), sb("moe_total", [P, NT], c)
        cwT = sb("moe_weightsT", [E, S], c)
        acc = sb("moe_acc", [P, NT, P], c)
        w_in = sem("moe_w_in", c)
        z_done, th_done, cw_done = sem("z_done", c), sem("th_done", c), sem("cw_done", c)
        y_done, self_v = sem("y_done", c), sem("moe_self_v", c)
        gate = Ring(c, nc, "gate", [psum[0]], 2 * B, 2 * B)
        hid = Ring(c, nc, "hid", psum[1:5], E * FC * B, E * FC * B)
        ye = Ring(c, nc, "ye", psum[5:7], E * B, E * B)
        dl = Ring(c, nc, "dl", [psum[7]], B, B)
        block = c.enter_context(nc.Block())

        @block.sync
        def _(sp):
            sp.dma_start(wg[:, :, :], ins["L1_ffn_Wg"].rearrange("r h e -> h r e")).then_inc(w_in, 16)
            sp.dma_start(bg[:, :, :], ins["L1_ffn_bg"].rearrange("(o r) e -> o r e", o=1).broadcast_to([P, R, E]))\
                .then_inc(w_in, 16)
            sp.dma_start(w1[:, :, :], ins["L1_ffn_W1"].rearrange("e h f -> h e f")).then_inc(w_in, 16)
            sp.dma_start(b1[:, :, :], ins["L1_ffn_b1"]).then_inc(w_in, 16)
            sp.dma_start(w2[:, :, :, :], ins["L1_ffn_W2"].rearrange("e (c p) h -> p e c h", p=P)).then_inc(w_in, 16)
            sp.dma_start(b2[:, :], ins["L1_ffn_b2"]).then_inc(w_in, 16)

        @block.tensor
        def _(pe):
            gate_c, hid_c, ye_c, dl_c = gate.cursor(), hid.cursor(), ye.cursor(), dl.cursor()

            def unit(r, b):
                i = r * B + b
                y = yT[:, b, 1:S + 1]
                if not (isinstance(r, int) and r == 0):
                    pe.wait_ge(y_done, i - B + 1)
                bank, q, full, free = gate_c.next()
                wait(pe, free, q)
                for t in range(NT):
                    last = nc.tensor.matmul(bank[:, t * E:(t + 1) * E], yT[:, b, 1 + t * P:1 + (t + 1) * P],
                                            wg[:, bass.ds(r, 1), :].rearrange("p o e -> p (o e)"), start=True, stop=True)
                last.then_inc(full, 1)
                moved = {}

                def hidden(e):
                    for f in range(FC):
                        bank, q, full, free = hid_c.next()
                        wait(pe, free, q)
                        nc.tensor.matmul(bank[:, :], w1[:, e, f * P:(f + 1) * P], y, start=True, stop=True)\
                            .then_inc(full, 1)
                        moved[e, f] = (free, q + 1)

                def outputs(e):
                    bank, q, full, free = ye_c.next()
                    for f in range(FC):
                        pe.wait_ge(*moved[e, f])
                    wait(pe, free, q)
                    for t in range(NT):
                        for f in range(FC):
                            last = nc.tensor.matmul(bank[:, t * P:(t + 1) * P], hm[:, e % 2, f, t * P:(t + 1) * P],
                                                    w2[:, e, f, :], start=(f == 0), stop=(f == FC - 1))
                    last.then_inc(full, 1)
                    return free, q + 1

                hidden(0)
                hidden(1)
                bank, q, full, free = gate_c.next()
                pe.wait_ge(cw_done, i + 1)
                for t in range(NT):
                    last = nc.tensor.transpose(bank[0:E, t * P:(t + 1) * P], cw[:, t, :], ident)
                last.then_inc(full, 1)
                weights = (free, q + 1)
                outputs(0)
                hidden(2)
                outputs(1)
                hidden(3)
                outputs(2)
                summed = outputs(3)
                bank, q, full, free = dl_c.next()
                wait(pe, y_done, i)
                pe.wait_ge(*weights)
                nc.tensor.matmul(bank[:, :], b2[:, :], cwT[:, :], start=True, stop=False, skip_group_check=True)
                pe.wait_ge(*summed)
                for t in range(NT):
                    last = nc.tensor.matmul(bank[:, t * P:(t + 1) * P], acc[:, t, :], ident, start=False,
                                            stop=(t == NT - 1), skip_group_check=True)
                last.then_inc(full, 1)

            def body(r):
                for cur in (gate_c, hid_c, ye_c, dl_c):
                    cur.begin(r)
                for b in range(B):
                    unit(r, b)
                for cur in (gate_c, hid_c, ye_c, dl_c):
                    cur.end()

            pe.wait_ge(w_in, 6 * 16)
            body(0)
            with pe.Fori(1, R) as r:
                body(r)

        @block.scalar
        def _(act):
            gate_c, hid_c, ye_c = gate.cursor(), hid.cursor(), ye.cursor()

            def unit(r, b):
                i = r * B + b
                gate_c.next()

                def hidden(e):
                    _, q, full, _ = ye_c.next()
                    wait(act, full, q)
                    for f in range(FC):
                        bank, q, full, free = hid_c.next()
                        act.wait_ge(full, q + 1)
                        nc.scalar.activation(hm[:, e % 2, f, :], bank[:, :], ACT.Gelu_apprx_tanh,
                                             bias=b1[:, e, f:f + 1]).then_inc(free, 1)

                hidden(0)
                act.wait_ge(z_done, i + 1)
                nc.scalar.activation(th[:, :, :], z[:, :, :], ACT.Tanh).then_inc(th_done, 1)
                hidden(1)
                bank, q, full, free = gate_c.next()
                act.wait_ge(full, q + 1)
                wait(act, y_done, i)
                nc.scalar.activation(cwT[:, :], bank[0:E, :], ACT.Copy).then_inc(free, 1)
                hidden(2)
                hidden(3)

            def body(r):
                for cur in (gate_c, hid_c, ye_c):
                    cur.begin(r)
                for b in range(B):
                    unit(r, b)
                for cur in (gate_c, hid_c, ye_c):
                    cur.end()

            act.wait_ge(w_in, 6 * 16)
            body(0)
            with act.Fori(1, R) as r:
                body(r)

        @block.vector
        def _(dve):
            LINKS = 9 * B
            chain = Chain(dve, self_v, LINKS, LINKS)
            gate_c, ye_c, dl_c = gate.cursor(), ye.cursor(), dl.cursor()

            def unit(r, b):
                i = r * B + b
                bank, q, full, free = gate_c.next()
                dve.wait_ge(full, q + 1)
                wait(dve, y_done, i)
                v = nc.vector
                v.tensor_tensor(lg[:, :, :], bank[:, 0:NT * E].rearrange("p (t e) -> p t e", e=E),
                                bg[:, bass.ds(r, 1), :].broadcast_to([P, NT, E]), ALU.add).then_inc(free, 1)
                dve.wait_ge(free, q + 1)
                mine = lg[:, :, :].unsqueeze(3).broadcast_to([P, NT, E, E])
                other = lg[:, :, :].unsqueeze(2).broadcast_to([P, NT, E, E])
                v.tensor_tensor(ge[:, :, :, :], other, mine, ALU.is_ge)
                chain.link(v.tensor_tensor(gt[:, :, :, :], other, mine, ALU.is_gt))
                chain.link(v.tensor_tensor(ge[:, :, :, :], ge[:, :, :, :], gt[:, :, :, :], ALU.subtract))
                first = table("before").rearrange("p (e f) -> p e f", f=E).unsqueeze(1).broadcast_to([P, NT, E, E])
                chain.link(v.tensor_tensor(ge[:, :, :, :], ge[:, :, :, :], first, ALU.mult))
                chain.link(v.tensor_tensor(ge[:, :, :, :], ge[:, :, :, :], gt[:, :, :, :], ALU.add))
                chain.link(v.tensor_reduce(rank[:, :, :], ge[:, :, :, :], X, ALU.add))
                chain.link(v.tensor_scalar(sel[:, :, :], rank[:, :, :], 1.5, None, ALU.is_lt))
                chain.link(v.tensor_tensor(sl[:, :, :], sel[:, :, :], lg[:, :, :], ALU.mult))
                chain.link(v.tensor_reduce(tot[:, :], sl[:, :, :], X, ALU.add))
                v.scalar_tensor_tensor(out=z[:, :, :], in0=tot[:, :].unsqueeze(2).broadcast_to([P, NT, E]), scalar=-0.5,
                                       in1=lg[:, :, :], op0=ALU.mult, op1=ALU.add).then_inc(z_done, 1)
                dve.wait_ge(th_done, i + 1)
                chain.link(v.scalar_tensor_tensor(out=th[:, :, :], in0=th[:, :, :], scalar=1.0, in1=sel[:, :, :],
                                                  op0=ALU.add, op1=ALU.mult))
                v.tensor_scalar(cw[:, :, :], th[:, :, :], 0.5, None, ALU.mult).then_inc(cw_done, 1)
                dve.wait_ge(cw_done, i + 1)
                gate_c.next()
                for e in range(E):
                    bank, q, full, free = ye_c.next()
                    dve.wait_ge(full, q + 1)
                    for t in range(NT):
                        y = bank[:, t * P:(t + 1) * P]
                        if e == 0:
                            last = v.tensor_scalar(acc[:, t, :], y, cw[:, t, e:e + 1], None, ALU.mult)
                        else:
                            last = v.scalar_tensor_tensor(out=acc[:, t, :], in0=y, scalar=cw[:, t, e:e + 1],
                                                          in1=acc[:, t, :], op0=ALU.mult, op1=ALU.add)
                    last.then_inc(free, 1)
                    dve.wait_ge(free, q + 1)
                bank, q, full, free = dl_c.next()
                dve.wait_ge(full, q + 1)
                ys = yT[:, b, 1:S + 1]
                v.tensor_tensor(ys, bank[:, :], ys, ALU.add).then_inc(y_done, 1)

            def body(r):
                chain.begin(r)
                for cur in (gate_c, ye_c, dl_c):
                    cur.begin(r)
                for b in range(B):
                    unit(r, b)
                chain.end()
                for cur in (gate_c, ye_c, dl_c):
                    cur.end()

            dve.wait_ge(w_in, 6 * 16)
            body(0)
            with dve.Fori(1, R) as r:
                body(r)
            dve.wait_ge(y_done, R * B)
            for b in range(B):
                nc.vector.tensor_tensor(xT[:, b, :], yT[:, b, 1:S + 1], xT[:, b, :], ALU.add)


def local(nc, ctx, o):
    sb, sem, ins, psum, xT, yT, ident, table, ones, mean_w = (
        o[k] for k in ("sb", "sem", "ins", "psum", "xT", "yT", "ident", "table", "ones", "mean_w"))
    with ExitStack() as c:
        def b_(n, shape, dt=F32):
            return sb("loc_" + n, shape, c, dt)

        def s_(n):
            return sem("loc_" + n, c)

        wqkv = b_("wqkv", [P, 2, 3 * H * DH])
        wo = b_("wo", [P, 8, P])
        w1 = b_("w1", [P, 2 * FI])
        w2 = b_("w2", [P, 3, P])
        scales = b_("scales", [P, DEPTH, 2, DH])
        tab = b_("tab", [P, DEPTH, 2, 2, NT, DH])
        vecs = b_("vecs", [P, 3, DEPTH])
        b1 = b_("b1", [P, DEPTH, 2, 3])
        xs = b_("xs", [P, 2, P])
        sq = b_("sq", [P, 2, 512])
        t2 = b_("t2", [P, 4, 8, DH])
        NQ = 4 * 8
        ss = b_("ss", [P, NQ + NT])
        yi, na = b_("yi", [P, NQ + NT]), b_("na", [P, NQ + NT])
        rn = b_("rn", [P, 2, NQ + NT])
        qk = b_("qk", [P, 2, 4, 512])
        qT = b_("qT", [P, 8, P])
        kT = b_("kT", [P, 2, 8, P])
        V = b_("V", [P, NT, H, DH])
        sm = b_("sm", [P, H, P + W])
        ex = b_("ex", [P, 2, H, P + W])
        mx = b_("mx", [P, H])
        rs, rr = b_("rs", [P, H]), b_("rr", [P, H])
        pT = b_("pT", [P, 4, 4, P])
        pTb = b_("pTb", [P, H, W])
        OT = b_("OT", [P, 8, P])
        s2, d2 = b_("s2", [P, S]), b_("d2", [P, S])
        xn = b_("xn", [P, S])
        diag = s2[:, :].rearrange("p (t n) -> p t n", t=NT)
        sq2 = xn
        gg = b_("gg", [P, 2, S])
        ag = [s2[:, :], d2[:, :], gg[:, 0, :]]
        tiny = b_("tiny", [P, B + 2])

        c_in = s_("c_in")
        wqkv_in, wo_in, wf_in = s_("wqkv_in"), s_("wo_in"), s_("wf_in")
        ready = s_("ready")
        xs_in, sq_in = s_("xs_in"), s_("sq_in")
        rot_in, rn_in = s_("rot_in"), s_("rn_in")
        qk_in = s_("qk_in")
        mx_in, ex_in = s_("mx_in"), s_("ex_in")
        rr_in, p_in = s_("rr_in"), s_("p_in")
        s2_in, sq2_in, r2_in, xn_in = s_("s2_in"), s_("sq2_in"), s_("r2_in"), s_("xn_in")
        xg_in = s_("xg_in")
        back_in = s_("back_in")
        f_done = s_("f_done")
        self_v, self_p = s_("self_v"), s_("self_p")
        proj = Ring(c, nc, "proj", psum[0:2], 24, 30)
        tr = Ring(c, nc, "tr", [psum[2], psum[6]], 20, 32)
        sc = Ring(c, nc, "sc", psum[3:5], 12, 16)
        bk = Ring(c, nc, "bk", [psum[5]], 6, 12)
        pv = Ring(c, nc, "pv", [psum[7]], 5, 16)

        def pv_before(i):
            return pv.first + (i - 1) * pv.steady

        def where(u, j, back):
            return (u, j - back) if j >= back else (u - 1, j - back + NT)

        def has(u, j, back):
            first, last = isinstance(u, int) and u == 0, isinstance(u, int) and u == UNITS
            return not (first and j < back) and not (last and j >= back)

        def steps(curs, engine_step):
            def iteration(u, nsteps=NT, check=True):
                for cur in curs:
                    cur.begin(u)
                for j in range(nsteps):
                    engine_step(u, j)
                if check:
                    for cur in curs:
                        cur.end()
            return iteration

        c1 = ExitStack()
        block = c1.enter_context(nc.Block())

        @block.sync
        def _(sp):
            for i, n in enumerate(("q_scale", "k_scale")):
                sp.dma_start(scales[:, :, i, :], ins["L0_ffn_" + n].rearrange("(o l) d -> o l d", o=1)
                             .broadcast_to([P, DEPTH, DH])).then_inc(c_in, 16)
            for i, n in enumerate(("ln_g", "ln_b", "b2")):
                sp.dma_start(vecs[:, i, :], ins["L0_ffn_" + n]).then_inc(c_in, 16)
            sp.dma_start(b1[:, :, :, :], ins["L0_ffn_b1"]).then_inc(c_in, 16)
            sp.wait_ge(c_in, 6 * 16)

        @block.vector
        def _(dve):
            nc.vector.memset(sm[:, :, P:P + W], NEG)
            dve.wait_ge(c_in, 6 * 16)
            rot = table("rot").rearrange("p (a c j d) -> p a c j d", a=2, c=2, j=NT)
            for a in range(2):
                def of(cs, lo, hi):
                    return rot[:, a, cs, :, lo:hi].unsqueeze(1).broadcast_to([P, DEPTH, NT, hi - lo])

                def by(lo, hi):
                    return scales[:, :, a, lo:hi].unsqueeze(2).broadcast_to([P, DEPTH, NT, hi - lo])
                nc.vector.tensor_tensor(tab[:, :, a, 0, :, :], of(0, 0, DH), by(0, DH), ALU.mult)
                hd = DH // 2
                nc.vector.tensor_tensor(tab[:, :, a, 1, :, 0:hd], of(1, 0, hd), by(hd, DH), ALU.mult)
                nc.vector.tensor_tensor(tab[:, :, a, 1, :, hd:DH], of(1, hd, DH), by(0, hd), ALU.mult)

        c1.close()
        block = c.enter_context(nc.Block())

        @block.sync
        def _(sp):
            def load_qkv(l, half):
                sp.dma_start(wqkv[:, half, :] if isinstance(half, int) else
                             wqkv[:, bass.ds(half, 1), :].rearrange("p o n -> p (o n)"),
                             ins["L0_ffn_Wqkv"][bass.ds(l, 1), :, :].rearrange("o p n -> p (o n)"))\
                    .then_inc(wqkv_in, 16)

            def load_wo(l):
                sp.dma_start(wo[:, :, :], ins["L0_ffn_Wo"][bass.ds(l, 1), :, :]
                             .rearrange("o (c p) n -> p (o c) n", p=P)).then_inc(wo_in, 16)

            def load_ffn(l):
                sp.dma_start(w1[:, :], ins["L0_ffn_W1"][bass.ds(l, 1), :, :].rearrange("o p n -> p (o n)"))\
                    .then_inc(wf_in, 16)
                src = ins["L0_ffn_W2"][bass.ds(l, 1), :, :]
                sp.dma_start(w2[:, 0:2, :], src[:, 0:2 * P, :].rearrange("o (c p) n -> p (o c) n", p=P))\
                    .then_inc(wf_in, 16)
                sp.dma_start(w2[0:FI - 2 * P, 2, :], src[:, 2 * P:FI, :].rearrange("o p n -> p (o n)"))\
                    .then_inc(wf_in, 16)

            def next_layer(l, more):
                if more:
                    sp.wait_ge(sq_in, l * (4 * NT * B) + 1)
                    load_qkv(l + 1, (l + 1) % 2)
                sp.wait_ge(pv.free[0], pv_before(l * B) + 7)
                load_wo(l)
                sp.wait_ge(f_done, l * B + B)
                load_ffn(l)

            load_qkv(0, 0)
            load_wo(0)
            load_ffn(0)
            sp.wait_ge(wqkv_in, 16)
            load_qkv(1, 1)
            with sp.Fori(1, DEPTH - 1) as l:
                next_layer(l, True)
            next_layer(DEPTH - 1, False)

        @block.tensor
        def _(pe):
            pj, tc, scc, bc, pc = proj.cursor(), tr.cursor(), sc.cursor(), bk.cursor(), pv.cursor()
            moved = {}

            def step(u, j):
                A = has(u, j, 0)
                Bm = has(u, j, 1)
                Ck = has(u, j, 2)
                F_ = not (isinstance(u, int) and u == 0)
                um, jm = where(u, j, 1)
                uk, jk = where(u, j, 2)
                n, m, k = u * NT + j, um * NT + jm, uk * NT + jk

                def project(s):
                    if not A:
                        return
                    if s == 0:
                        if j == 0:
                            pe.wait_ge(wqkv_in, (u // B) * 16 + 16)
                        pe.wait_ge(xs_in, 2 * n + 2)
                    at = (s % 2) * H * DH + (s // 2) * 512 if s < 4 else 2 * H * DH + (s - 4) * 512
                    bank, q, full, free = pj.next()
                    wait(pe, free, q)
                    half = (u // B) % 2
                    rhs = wqkv[:, half, at:at + 512] if isinstance(half, int) else \
                        wqkv[:, bass.ds(half, 1), at:at + 512].rearrange("p o n -> p (o n)")
                    nc.tensor.matmul(bank[:, :], xs[:, j % 2, :], rhs, start=True, stop=True).then_inc(full, 1)

                def turn_p(g):
                    if not Ck:
                        return
                    bank, q, full, free = tc.next()
                    pe.wait_ge(p_in, 2 * k + g // 2 + 1)
                    wait(pe, free, q)
                    for i in range(4):
                        last = nc.tensor.transpose(bank[:, i * P:(i + 1) * P], ex[:, jk % 2, 4 * g + i, 0:P], ident)
                    last.then_inc(full, 1)
                    moved["p", g] = (free, q + 1)

                def turn_back(r):
                    if not Ck or jk == 0:
                        return
                    bank, q, full, free = bc.next()
                    pe.wait_ge(p_in, 2 * k + r + 1)
                    wait(pe, free, q)
                    for i in range(8):
                        last = nc.tensor.matmul(bank[P - W:P, i * W:(i + 1) * W], ex[:, jk % 2, 8 * r + i, P:P + W],
                                                ident[:, 0:W], start=True, stop=True)
                    last.then_inc(full, 1)
                    moved["b", r] = (free, q + 1)

                def outputs(r):
                    if not Ck:
                        return
                    bank, q, full, free = pc.next()
                    for e in range(2):
                        pe.wait_ge(*moved["p", 2 * r + e])
                    if jk > 0:
                        pe.wait_ge(*moved["b", r])
                    wait(pe, free, q)
                    for e in range(2):
                        lo, hi = 64 * e, 64 * e + 64
                        for i in range(4):
                            h = 8 * r + 2 * i + e
                            last = nc.tensor.matmul(bank[lo:hi, i * P:(i + 1) * P], V[:, jk, h, :], pT[:, 2 * r + e, i, :],
                                                    start=True, stop=(jk == 0))
                            if jk > 0:
                                last = nc.tensor.matmul(bank[lo:hi, i * P:i * P + W], V[P - W:P, jk - 1, h, :],
                                                        pTb[P - W:P, 8 * r + 4 * e + i, :], start=False, stop=True)
                    last.then_inc(full, 1)

                def turn_qk(s):
                    if not Bm:
                        return
                    bank, q, full, free = tc.next()
                    pe.wait_ge(qk_in, 4 * m + s + 1)
                    wait(pe, free, q)
                    for i in range(4):
                        last = nc.tensor.transpose(bank[:, i * P:(i + 1) * P], qk[:, jm % 2, s, i * P:(i + 1) * P], ident)
                    last.then_inc(full, 1)
                    moved["q", s] = (free, q + 1)

                def scores(r):
                    if not Bm:
                        return
                    for s in (2 * r, 2 * r + 1):
                        pe.wait_ge(*moved["q", s])
                    jobs = [scc.next() for e in range(2)]

                    def back(e, bank):
                        lo, hi = 64 * e, 64 * e + 64
                        for i in range(4):
                            at = e * P + i * W
                            last = nc.tensor.matmul(bank[0:W, at:at + W], qT[lo:hi, 4 * r + i, 0:W],
                                                    kT[lo:hi, 1 - jm % 2, 4 * r + i, P - W:P], start=True, stop=True)
                        return last

                    if jm > 0:
                        bank, q, full, free = bc.next()
                        wait(pe, free, q)
                    for e in range(2):
                        wait(pe, jobs[e][3], jobs[e][1])
                    for i in range(4):
                        if i == 2 and jm > 0:
                            back(0, bank).then_inc(back_in, 1)
                        if i == 3 and jm > 0:
                            pe.wait_ge(back_in, 2 * (NT - 1) * um + 2 * (jm - 1) + r + 1)
                        for e in range(2):
                            lo, hi = 64 * e, 64 * e + 64
                            last = nc.tensor.matmul(jobs[e][0][:, i * P:(i + 1) * P], qT[lo:hi, 4 * r + i, :],
                                                    kT[lo:hi, jm % 2, 4 * r + i, :], start=True, stop=True)
                            if i == 3:
                                last.then_inc(jobs[e][2], 1)
                    if jm > 0:
                        back(1, bank).then_inc(full, 1)

                def project_out():
                    if not has(u, j, 3):
                        return
                    uo, jo = where(u, j, 3)
                    if jo == 0:
                        pe.wait_ge(wo_in, (uo // B) * 16 + 16)
                    bank, q, full, free = pc.next()
                    pe.wait_ge(free, q)
                    for cc in range(8):
                        last = nc.tensor.matmul(bank[:, 0:P], wo[:, cc, :], OT[:, cc, :], start=(cc == 0), stop=(cc == 7))
                    last.then_inc(full, 1)

                def ffn_mean():
                    pe.wait_ge(s2_in, u)
                    bank, q, full, free = pc.next()
                    pe.wait_ge(free, q)
                    nc.tensor.matmul(bank[:, :], mean_w[:, :], s2[:, :], start=True, stop=True).then_inc(full, 1)

                def ffn_var():
                    pe.wait_ge(sq2_in, u)
                    bank, q, full, free = pc.next()
                    pe.wait_ge(free, q)
                    for t in range(NT):
                        last = nc.tensor.matmul(bank[:, t:t + 1], sq2[:, t * P:(t + 1) * P], mean_w[:, 0:1],
                                                start=True, stop=True)
                    last.then_inc(full, 1)

                def ffn_spread():
                    pe.wait_ge(r2_in, u)
                    bank, q, full, free = pc.next()
                    pe.wait_ge(free, q)
                    nc.tensor.matmul(bank[:, :], ones[:, :], diag[:, :, :].rearrange("p t n -> p (t n)"),
                                     start=True, stop=True).then_inc(full, 1)

                def ffn_up(i, part):
                    if i == 0 and part == 1:
                        pe.wait_ge(xn_in, u)
                        pe.wait_ge(wf_in, ((u - 1) // B) * 48 + 48)
                    lo, w = FCH[i]
                    bank, q, full, free = pj.next()
                    pe.wait_ge(free, q)
                    nc.tensor.matmul(bank[0:w, :], w1[:, part * FI + lo:part * FI + lo + w], xn[:, :],
                                     start=True, stop=True).then_inc(full, 1)
                    moved["f", i] = (free, q + 1)

                def ffn_down():
                    bank, q, full, free = pc.next()
                    for i in range(3):
                        pe.wait_ge(*moved["f", i])
                    pe.wait_ge(free, q)
                    for i, (lo, w) in enumerate(FCH):
                        last = nc.tensor.matmul(bank[:, :], w2[0:w, i, :], ag[i][0:w], start=(i == 0), stop=(i == 2))
                    last.then_inc(full, 1)

                up = F_ and j == 3
                project(0)
                project(1)
                if up:
                    ffn_spread()
                turn_qk(0)
                turn_qk(1)
                project_out()
                project(2)
                scores(0)
                if F_ and j == 2:
                    ffn_mean()
                project(3)
                turn_qk(2)
                turn_qk(3)
                turn_p(0)
                turn_p(1)
                turn_back(0)
                if F_ and j == 2:
                    ffn_var()
                project(4)
                scores(1)
                if up:
                    ffn_up(0, 1)
                    ffn_up(0, 0)
                outputs(0)
                if up:
                    project(5)
                turn_p(2)
                if up:
                    ffn_up(1, 1)
                    ffn_up(1, 0)
                turn_back(1)
                turn_p(3)
                if up:
                    ffn_up(2, 1)
                    ffn_up(2, 0)
                    outputs(1)
                    ffn_down()
                else:
                    project(5)
                    outputs(1)

            curs = (pj, tc, scc, bc, pc)
            it = steps(curs, step)
            it(0)
            with pe.Fori(1, UNITS) as u:
                it(u)
            it(UNITS, check=False)

        @block.scalar
        def _(act):
            pj, tc, bc, pc = proj.cursor(), tr.cursor(), bk.cursor(), pv.cursor()

            def step(u, j):
                A, Bm, Ck = has(u, j, 0), has(u, j, 1), has(u, j, 2)
                F_ = not (isinstance(u, int) and u == 0)
                um, jm = where(u, j, 1)
                uk, jk = where(u, j, 2)
                n, m, k = u * NT + j, um * NT + jm, uk * NT + jk

                def square(s):
                    if not A:
                        return
                    bank, q, full, free = pj.next()
                    act.wait_ge(full, q + 1)
                    wait(act, rot_in, 4 * n + s - 1)
                    nc.scalar.activation(sq[:, s % 2, :], bank[:, :], ACT.Square).then_inc(sq_in, 1)

                def values(s):
                    if not A:
                        return
                    bank, q, full, free = pj.next()
                    act.wait_ge(full, q + 1)
                    nc.scalar.activation(V[:, j, 8 * s:8 * s + 8, 0:DH], bank[:, :].rearrange("p (h d) -> p h d", d=DH),
                                         ACT.Copy).then_inc(free, 1)

                def move(dst, on=True):
                    if not on:
                        return
                    bank, q, full, free = tc.next()
                    act.wait_ge(full, q + 1)
                    nc.scalar.activation(dst, bank[:, :], ACT.Copy).then_inc(free, 1)

                def move_p(g):
                    move(pT[:, g, :, :].rearrange("p i t -> p (i t)"), Ck)

                def move_back(r):
                    if not Ck or jk == 0:
                        return
                    bank, q, full, free = bc.next()
                    act.wait_ge(full, q + 1)
                    nc.scalar.activation(pTb[P - W:P, 8 * r:8 * r + 8, 0:W],
                                         bank[P - W:P, 0:8 * W].rearrange("p (i t) -> p i t", t=W), ACT.Copy).then_inc(free, 1)

                def move_o(r):
                    if not Ck:
                        return
                    bank, q, full, free = pc.next()
                    act.wait_ge(full, q + 1)
                    nc.scalar.activation(OT[:, 4 * r:4 * r + 4, :].rearrange("p i t -> p (i t)"), bank[:, :], ACT.Copy)\
                        .then_inc(free, 1)

                def move_qk(s):
                    r = s // 2
                    dst = kT[:, jm % 2, 4 * r:4 * r + 4, :] if s % 2 else qT[:, 4 * r:4 * r + 4, :]
                    move(dst.rearrange("p i t -> p (i t)"), Bm)

                def exponentials(t, jt, r, quarter, on):
                    if not on:
                        return
                    w = P + W if jt > 0 else P
                    if quarter == 0:
                        act.wait_ge(mx_in, 2 * t + r + 1)
                    at = 8 * r + 4 * quarter
                    for i in range(at, at + 4):
                        last = nc.scalar.activation(ex[:, jt % 2, i, 0:w], sm[:, i, 0:w], ACT.Exp, bias=mx[:, i:i + 1],
                                                    accum_out=rs[:, i:i + 1])
                    if quarter == 1:
                        last.then_inc(ex_in, 1)

                up = F_ and j == 3

                def ffn_square():
                    bank, q, full, free = pc.next()
                    act.wait_ge(free, q + 1)
                    nc.scalar.activation(sq2[:, :], d2[:, :], ACT.Square).then_inc(sq2_in, 1)

                def ffn_gelu(i):
                    lo, w = FCH[i]
                    bank, q, full, free = pj.next()
                    act.wait_ge(full, q + 1)
                    if i == 2:
                        act.wait_ge(*gated[0])
                    nc.scalar.activation(gg[0:w, i % 2, :], bank[0:w, :], ACT.Gelu,
                                         bias=b1[0:w, bass.ds((u - 1) // B, 1), 1, i:i + 1].rearrange("p a b -> p (a b)"))\
                        .then_inc(free, 1)
                    _, q, _, free = pj.next()
                    gated[i] = (free, q + 1)

                gated = {}
                square(0)
                square(1)
                if up:
                    pc.next()
                move_qk(0)
                move_qk(1)
                if has(u, j, 3):
                    pc.next()
                if up:
                    act.wait_ge(xg_in, u)
                    nc.scalar.activation(xn[:, :], d2[:, :], ACT.Identity,
                                         bias=vecs[:, 1, bass.ds((u - 1) // B, 1)]).then_inc(xn_in, 1)
                exponentials(k, jk, 1, 0, Ck)
                square(2)
                exponentials(k, jk, 1, 1, Ck)
                square(3)
                move_qk(2)
                if F_ and j == 2:
                    ffn_square()
                    pc.next()
                move_qk(3)
                if Bm and jm > 0:
                    bc.next()
                move_p(0)
                move_p(1)
                move_back(0)
                values(0)
                exponentials(m, jm, 0, 0, Bm)
                if Bm and jm > 0:
                    bc.next()
                if up:
                    exponentials(m, jm, 0, 1, Bm)
                    ffn_gelu(0)
                move_o(0)
                if up:
                    values(1)
                move_p(2)
                if up:
                    ffn_gelu(1)
                move_back(1)
                move_p(3)
                if up:
                    ffn_gelu(2)
                    move_o(1)
                    pc.next()
                else:
                    values(1)
                    exponentials(m, jm, 0, 1, Bm)
                    move_o(1)

            it = steps((pj, tc, bc, pc), step)
            it(0)
            with act.Fori(1, UNITS) as u:
                it(u)
            it(UNITS, check=False)

        @block.vector
        def _(dve):
            pj, scc, bc, pc = proj.cursor(), sc.cursor(), bk.cursor(), pv.cursor()
            chain = Chain(dve, self_v, NT * 11, NT * 11)
            v = nc.vector

            def rsqrt(y, yint, a, x, done):
                chain.link(v.tensor_scalar(yint, x.bitcast(I32), 1, None, ALU.arith_shift_right))
                chain.link(v.tensor_scalar(yint, yint, -1.0, float(MAGIC), ALU.mult, ALU.add))
                yf = yint.bitcast(F32)
                for i in range(3):
                    chain.link(v.scalar_tensor_tensor(out=a, in0=yf, scalar=-0.5, in1=yf, op0=ALU.mult, op1=ALU.mult))
                    chain.link(v.tensor_tensor(a, a, x, ALU.mult))
                    dst = y if i == 2 else yf
                    last = v.scalar_tensor_tensor(out=dst, in0=a, scalar=1.5, in1=yf, op0=ALU.add, op1=ALU.mult)
                    if i < 2:
                        chain.link(last)
                    else:
                        last.then_inc(done, 1)

            def step(u, j):
                A, Bm, Ck = has(u, j, 0), has(u, j, 1), has(u, j, 2)
                F_ = not (isinstance(u, int) and u == 0)
                um, jm = where(u, j, 1)
                uk, jk = where(u, j, 2)
                n, m, k = u * NT + j, um * NT + jm, uk * NT + jk
                up = F_ and j == 3
                lf = bass.ds((u - 1) // B, 1)

                def rotate(s):
                    if not A:
                        return
                    bank, q, full, free = pj.next()
                    dve.wait_ge(sq_in, 4 * n + s + 1)
                    wait(dve, qk_in, 4 * n + s - 3)
                    x3 = bank[:, :].rearrange("p (h d) -> p h d", d=DH)
                    x4 = bank[:, :].rearrange("p (h a d) -> p h a d", a=2, d=DH // 2)
                    tb = tab[:, bass.ds(u // B, 1), s % 2, :, j, :].rearrange("p o c d -> p (o c) d")
                    v.tensor_tensor(qk[:, j % 2, s, :].rearrange("p (h d) -> p h d", d=DH), x3, tb[:, 0, :].unsqueeze(1).broadcast_to([P, 8, DH]), ALU.mult)
                    v.tensor_tensor(t2[:, s, :, :].rearrange("p h (a d) -> p h a d", a=2), x4[:, :, ::-1, :],
                                    tb[:, 1, :].rearrange("p (a d) -> p a d", a=2).unsqueeze(1)
                                    .broadcast_to([P, 8, 2, DH // 2]), ALU.mult).then_inc(free, 1)
                    v.tensor_reduce(ss[:, 8 * s:8 * s + 8], sq[:, s % 2, :].rearrange("p (h d) -> p h d", d=DH), X, ALU.add)\
                        .then_inc(rot_in, 1)

                def norms():
                    var = F_ and j == 2
                    if not A and not var:
                        return
                    lo, hi = (0 if A else NQ), (NQ + NT if var else NQ)
                    if var:
                        bank, q, full, free = var_job
                        dve.wait_ge(full, q + 1)
                        v.tensor_scalar(ss[:, NQ:NQ + NT], bank[:, 0:NT], EPS, None, ALU.add).then_inc(free, 1)
                        dve.wait_ge(free, q + 1)
                    if A:
                        dve.wait_ge(rot_in, 4 * n + 4)
                        wait(dve, qk_in, 4 * (n - 1))
                    chain.link(v.tensor_scalar(ss[:, lo:hi], ss[:, lo:hi], 1e-24, None, ALU.max))
                    rsqrt(rn[:, j % 2, lo:hi], yi[:, lo:hi].bitcast(I32), na[:, lo:hi], ss[:, lo:hi], rn_in)
                    if var:
                        dve.wait_ge(rn_in, n + 1 if A else UNITS * NT + 1)
                        v.tensor_tensor(diag[:, :, :], ident.unsqueeze(1).broadcast_to([P, NT, P]),
                                        rn[:, j % 2, NQ:NQ + NT].unsqueeze(2).broadcast_to([P, NT, P]), ALU.mult)\
                            .then_inc(r2_in, 1)

                def inverse(t, r, on):
                    if not on:
                        return
                    dve.wait_ge(ex_in, 2 * t + r + 1)
                    wait(dve, p_in, 2 * t + r - 1)
                    v.reciprocal(rr[:, 8 * r:8 * r + 8], rs[:, 8 * r:8 * r + 8]).then_inc(rr_in, 1)

                def maxima(r):
                    if not Bm:
                        return
                    w = P + W if jm > 0 else P
                    wait(dve, ex_in, 2 * (m - 1) + r + 1)
                    for e in range(2):
                        bank, q, full, free = scc.next()
                        dve.wait_ge(full, q + 1)
                        v.tensor_tensor(sm[:, 8 * r + 4 * e:8 * r + 4 * e + 4, 0:P],
                                        bank[:, :].rearrange("p (i t) -> p i t", t=P),
                                        table("band").unsqueeze(1).broadcast_to([P, 4, P]), ALU.add).then_inc(free, 1)
                        own = (free, q + 1)
                    if jm > 0:
                        bank, q, full, free = bc.next()
                        dve.wait_ge(full, q + 1)
                        v.tensor_tensor(sm[0:W, 8 * r:8 * r + 8, P:P + W],
                                        bank[0:W, 0:8 * W].rearrange("p (i t) -> p i t", t=W),
                                        table("back")[0:W, :].unsqueeze(1).broadcast_to([W, 8, W]), ALU.add)\
                            .then_inc(free, 1)
                        own = (free, q + 1)
                    dve.wait_ge(*own)
                    v.tensor_reduce(mx[:, 8 * r:8 * r + 8], sm[:, 8 * r:8 * r + 8, 0:w], X, ALU.max,
                                    negate=True).then_inc(mx_in, 1)

                def add_attention():
                    if not has(u, j, 3):
                        return
                    uo, jo = where(u, j, 3)
                    bank, q, full, free = pc.next()
                    dve.wait_ge(full, q + 1)
                    y = yT[:, bass.ds(uo % B, 1), 1 + jo * P:1 + (jo + 1) * P].rearrange("p o t -> p (o t)")
                    v.tensor_tensor(y, bank[:, 0:P], y, ALU.add).then_inc(free, 1)
                    if jo == NT - 1:
                        dve.wait_ge(free, q + 1)
                        src = yT[:, bass.ds((u - 1) % B, 1), :].rearrange("p o t -> p (o t)")
                        v.tensor_copy(s2[0:P // 2, :], src[0:P // 2, 1:S + 1])
                        v.tensor_copy(s2[P // 2:P, :], src[P // 2:P, 0:S]).then_inc(s2_in, 1)

                def ffn_centre():
                    bank, q, full, free = pc.next()
                    dve.wait_ge(full, q + 1)
                    v.tensor_tensor(d2[:, :], s2[:, :], bank[:, :], ALU.subtract).then_inc(free, 1)

                def ffn_norm():
                    bank, q, full, free = pc.next()
                    dve.wait_ge(full, q + 1)
                    v.scalar_tensor_tensor(out=d2[:, :], in0=d2[:, :], scalar=vecs[:, 0, lf], in1=bank[:, :],
                                           op0=ALU.mult, op1=ALU.mult).then_inc(free, 1)
                    dve.wait_ge(free, q + 1)
                    v.memset(tiny[:, B:B + 1], 0.0).then_inc(xg_in, 1)

                def ffn_gate(i):
                    lo, w = FCH[i]
                    _, q, _, free = pj.next()
                    dve.wait_ge(free, q + 1)
                    bank, q, full, free = pj.next()
                    dve.wait_ge(full, q + 1)
                    v.scalar_tensor_tensor(out=ag[i][0:w], in0=bank[0:w, :],
                                           scalar=b1[0:w, lf, 0, i:i + 1].rearrange("p a b -> p (a b)"),
                                           in1=gg[0:w, i % 2, :], op0=ALU.add, op1=ALU.mult).then_inc(free, 1)

                def ffn_add():
                    bank, q, full, free = pc.next()
                    dve.wait_ge(full, q + 1)
                    y = yT[:, bass.ds((u - 1) % B, 1), 1:S + 1].rearrange("p o t -> p (o t)")
                    v.scalar_tensor_tensor(out=y, in0=bank[:, :], scalar=vecs[:, 2, lf], in1=y,
                                           op0=ALU.add, op1=ALU.add).then_inc(free, 1)
                    dve.wait_ge(free, q + 1)
                    v.memset(tiny[:, B + 1:B + 2], 0.0).then_inc(f_done, 1)

                if up:
                    ffn_norm()
                rotate(0)
                inverse(k, 0, Ck)
                rotate(1)
                add_attention()
                rotate(2)
                inverse(k, 1, Ck)
                if F_ and j == 2:
                    ffn_centre()
                maxima(0)
                if Ck and jk > 0:
                    bc.next()
                rotate(3)
                if F_ and j == 2:
                    var_job = pc.next()
                if Ck:
                    pc.next()
                    pc.next()
                if A:
                    pj.next()
                norms()
                if up:
                    ffn_gate(0)
                if A:
                    pj.next()
                maxima(1)
                if Ck and jk > 0:
                    bc.next()
                if up:
                    ffn_gate(1)
                    ffn_gate(2)
                if up:
                    ffn_add()

            for b in range(B):
                v.memset(tiny[:, b:b + 1], 0.0).then_inc(f_done, 1)
            it = steps((pj, scc, bc, pc, chain), step)
            it(0)
            with dve.Fori(1, UNITS) as u:
                it(u)
            it(UNITS, check=False)
            dve.wait_ge(f_done, B + UNITS)
            for b in range(B):
                v.tensor_tensor(xT[:, b, :], yT[:, b, 1:S + 1], xT[:, b, :], ALU.add)

        @block.gpsimd
        def _(pool):
            chain = Chain(pool, self_p, 4 * NT, 4 * NT)
            g = nc.gpsimd

            def shifted(dst, b, at, width, done, before):
                hc = P // 2
                src = yT[:, bass.ds(b, 1), :].rearrange("p o t -> p (o t)") if not isinstance(b, int) else yT[:, b, :]
                g.tensor_copy(dst[0:hc, :], src[0:hc, at + 1:at + 1 + width]).then_inc(done, 1)
                pool.wait_ge(done, 2 * before + 1)
                g.tensor_copy(dst[hc:P, :], src[hc:P, at:at + width]).then_inc(done, 1)
                pool.wait_ge(done, 2 * before + 2)

            def step(u, j):
                A, Bm, Ck = has(u, j, 0), has(u, j, 1), has(u, j, 2)
                F_ = not (isinstance(u, int) and u == 0)
                um, jm = where(u, j, 1)
                uk, jk = where(u, j, 2)
                n, m, k = u * NT + j, um * NT + jm, uk * NT + jk

                def join(s):
                    if not A:
                        return
                    pool.wait_ge(rot_in, 4 * n + s + 1)
                    x = qk[:, j % 2, s, :].rearrange("p (h d) -> p h d", d=DH)
                    chain.link(g.tensor_tensor(x, x, t2[:, s, :, :], ALU.add))

                def normalise(s):
                    if not A:
                        return
                    pool.wait_ge(rn_in, n + 1)
                    x = qk[:, j % 2, s, :].rearrange("p (h d) -> p h d", d=DH)
                    g.tensor_tensor(x, x, rn[:, j % 2, 8 * s:8 * s + 8].unsqueeze(2).broadcast_to([P, 8, DH]), ALU.mult)\
                        .then_inc(qk_in, 1)

                def next_input():
                    if not A:
                        return
                    un, jn = (u, j + 1) if j < NT - 1 else (u + 1, 0)
                    pool.wait_ge(sq_in, 4 * n + 1)
                    if jn == 0:
                        pool.wait_ge(f_done, un + 1)
                    shifted(xs[:, jn % 2, :], un % B, jn * P, P, xs_in, n + 1)

                def probabilities(r):
                    if not Ck:
                        return
                    w = P + W if jk > 0 else P
                    pool.wait_ge(rr_in, 2 * k + r + 1)
                    e = ex[:, jk % 2, 8 * r:8 * r + 8, 0:w]
                    g.tensor_tensor(e, e, rr[:, 8 * r:8 * r + 8].unsqueeze(2).broadcast_to([P, 8, w]), ALU.mult)\
                        .then_inc(p_in, 1)

                join(0)
                probabilities(0)
                join(1)
                probabilities(1)
                next_input()
                join(2)
                join(3)
                for s in range(4):
                    normalise(s)

            pool.wait_ge(f_done, 1)
            shifted(xs[:, 0, :], 0, 0, P, xs_in, 0)
            it = steps((chain,), step)
            it(0)
            with pool.Fori(1, UNITS) as u:
                it(u)
            it(UNITS, check=False)


def net(nc, ins, out, consts, place, phases="ABCD"):
    ctx = ExitStack()
    with ctx:
        def sb(name, shape, c=ctx, dt=F32):
            return c.enter_context(nc.sbuf_tensor(name, shape, dt))

        def sem(name, c=ctx):
            return c.enter_context(nc.semaphore(name))

        xT = sb("xT", [P, B, S])
        yT = sb("yT", [P, B, S + 1])
        cst = sb("cst", [P, consts.shape[1]])
        ones = sb("ones", [P, P])
        mean_w = sb("mean_w", [P, P])
        eps = sb("eps", [P, 1])
        ctxT = sb("ctxT", [P, B, SK])
        psum = [ctx.enter_context(nc.psum_tensor(f"bank{i}", [P, 512], F32)) for i in range(8)]

        def table(name):
            at, n = place[name]
            return cst[:, at:at + n]

        ident = table("ident")

        layernorm_count = [0]

        def layernorm(src, dst):
            n = layernorm_count[0]
            layernorm_count[0] += 1
            with ExitStack() as c:
                d = sb(f"ln_d{n}", [P, B, S], c)
                sq = sb(f"ln_sq{n}", [P, B, S], c)
                sd = sb(f"ln_sd{n}", [P, B, S], c)
                rs = sb(f"ln_rs{n}", [P, B, S], c)
                mean_done, d_done = sem(f"mean_done{n}", c), sem(f"d_done{n}", c)
                sq_done, var_done = sem(f"sq_done{n}", c), sem(f"var_done{n}", c)
                sd_done, rs_done = sem(f"sd_done{n}", c), sem(f"rs_done{n}", c)
                block = c.enter_context(nc.Block())

                @block.tensor
                def _(pe):
                    for b in range(B):
                        nc.tensor.matmul(psum[b][:, :], mean_w[:, :], src(b), start=True, stop=True)\
                            .then_inc(mean_done, 1)
                    for b in range(B):
                        pe.wait_ge(sq_done, b + 1)
                        nc.tensor.matmul(psum[4 + b][:, :], mean_w[:, :], sq[:, b, :], start=True, stop=True)\
                            .then_inc(var_done, 1)

                @block.scalar
                def _(act):
                    for b in range(B):
                        act.wait_ge(d_done, b + 1)
                        nc.scalar.activation(sq[:, b, :], d[:, b, :], ACT.Square).then_inc(sq_done, 1)
                    for b in range(B):
                        act.wait_ge(var_done, b + 1)
                        nc.scalar.activation(sd[:, b, :], psum[4 + b][:, :], ACT.Sqrt, bias=eps[:, 0:1])\
                            .then_inc(sd_done, 1)

                @block.vector
                def _(dve):
                    for b in range(B):
                        dve.wait_ge(mean_done, b + 1)
                        nc.vector.tensor_tensor(d[:, b, :], src(b), psum[b][:, :], ALU.subtract)\
                            .then_inc(d_done, 1)
                    for b in range(B):
                        dve.wait_ge(sd_done, b + 1)
                        nc.vector.reciprocal(rs[:, b, :], sd[:, b, :]).then_inc(rs_done, 1)
                    for b in range(B):
                        dve.wait_ge(rs_done, b + 1)
                        nc.vector.tensor_tensor(dst(b), d[:, b, :], rs[:, b, :], ALU.mult)

        with ExitStack() as c:
            xtok = sb("xtok", [P, B * NT, P], c)
            ctok = sb("ctok", [SK, B, P], c)
            x_in, c_in, k_in = sem("x_in", c), sem("c_in", c), sem("k_in", c)
            xt_full, xt_done = sem("xt_full", c), sem("xt_done", c)
            block = c.enter_context(nc.Block())

            @block.sync
            def _(sp):
                sp.dma_start(cst[:, :], consts).then_inc(k_in, 16)
                sp.dma_start(xtok[:, :, :], ins["x"].rearrange("b (t p) d -> p (b t) d", p=P)).then_inc(x_in, 16)
                sp.dma_start(ctok[:, :, :], ins["ctx_1024"].rearrange("b s d -> s b d")).then_inc(c_in, 16)

            @block.vector
            def _(dve):
                nc.vector.memset(ones[:, :], 1.0)
                nc.vector.memset(mean_w[:, :], 1.0 / P)
                nc.vector.memset(eps[:, :], EPS)
                nc.vector.memset(yT[:, :, 0:1], 0.0)

            @block.tensor
            def _(pe):
                pe.wait_ge(k_in, 16)
                pe.wait_ge(x_in, 16)
                for b in range(B):
                    for t in range(NT):
                        last = nc.tensor.transpose(psum[b][:, t * P:(t + 1) * P], xtok[:, b * NT + t, :], ident)
                    last.then_inc(xt_full, 1)
                pe.wait_ge(c_in, 16)
                for b in range(B):
                    last = nc.tensor.transpose(psum[4][:, b * SK:(b + 1) * SK], ctok[:, b, :], ident[0:SK, 0:SK])
                last.then_inc(xt_full, 1)

            @block.scalar
            def _(act):
                for b in range(B):
                    act.wait_ge(xt_full, b + 1)
                    nc.scalar.activation(xT[:, b, :], psum[b][:, :], ACT.Copy)
                act.wait_ge(xt_full, B + 1)
                nc.scalar.activation(ctxT[:, :, :], psum[4][:, 0:B * SK].rearrange("p (b s) -> p b s", s=SK), ACT.Copy)

        def x_of(b):
            return xT[:, b, :]

        def y_of(b):
            return yT[:, b, 1:S + 1]

        def cross(kind):
            first = kind == "A"
            scale = 8.0 ** -0.5 if first else 64.0 ** -0.5
            with ExitStack() as c:
                def s_(n):
                    return sem(f"{kind}_{n}", c)

                def b_(n, shape, dt=F32):
                    return sb(f"{kind}_{n}", shape, c, dt)

                w_in = s_("w_in")
                wt_full, wt_done = s_("wt_full"), s_("wt_done")
                kv_full, kv_done = s_("kv_full"), s_("kv_done")
                kT, vT = b_("kT", [P, B, SK]), b_("vT", [P, B, SK])
                if first:
                    wq, wk, wv, wo = (b_(n, [P, P]) for n in ("wq", "wk", "wv", "wo"))
                    bias = b_("bias", [P, 4])
                    wkT, wvT, woT = (b_(n, [P, P]) for n in ("wkT", "wvT", "woT"))
                    bq_rep = b_("bq_rep", [P, P])
                    wo_heads = b_("wo_heads", [P, H, P])
                    mask8 = b_("mask8", [P, B, SK], mybir.dt.uint8)
                    maskf = b_("maskf", [P, B, SK])
                    kv, vv = b_("kv", [P, H, SK]), b_("vv", [P, SK])
                    mask_b = b_("mask_b", [P, H, SK])
                else:
                    wq, wqT = b_("wq", [P, H * DH]), b_("wqT", [P, 8, P])
                    wk2, wv2 = b_("wk2", [P, 2, DH]), b_("wv2", [P, 2, DH])
                    wo = b_("wo", [P, 8, P])
                    kv, vv = b_("kv", [P, 2, SK]), b_("vv", [P, 2, SK])
                G = b_("G", [P, H, SK])
                U = b_("U", [SK, H, P])
                xs = b_("xs", [P, 2, P])
                sm = b_("sm", [P, 2, H, SK])
                ex = b_("ex", [P, NT, H, SK])
                mx, den, rden = b_("mx", [P, 2, H]), b_("den", [P, H]), b_("rden", [P, 2, H])
                pT = b_("pT", [SK, 2, H, P])

                kv_in, vv_in = s_("kv_in"), s_("vv_in")
                xs_in = s_("xs_in")
                sc_full, sc_done = s_("sc_full"), s_("sc_done")
                mx_done, sub_done = s_("mx_done"), s_("sub_done")
                ex_done, rd_done = s_("ex_done"), s_("rd_done")
                p_done = s_("p_done")
                o_full, o_done = s_("o_full"), s_("o_done")
                self_v = s_("self_v")
                GJ = HJ if first else [(0, 4), (4, 4), (8, 4), (12, 4)]
                NG = 2 * len(GJ) if first else len(GJ)
                prep = Ring(c, nc, f"{kind}_prep", [psum[5], psum[6]], NG + 4 + NG, 4 + NG)
                pt = Ring(c, nc, f"{kind}_pt", [psum[3], psum[4]], 8, 16)

                c1 = ExitStack()
                block = c1.enter_context(nc.Block())

                @block.sync
                def _(sp):
                    if first:
                        for t, n in ((wq, "w_q"), (wk, "w_k"), (wv, "w_v"), (wo, "w_o")):
                            sp.dma_start(t[:, :], ins["L0_xattn_" + n]).then_inc(w_in, 16)
                        for i, n in enumerate(("b_q", "b_k", "b_v", "b_o")):
                            sp.dma_start(bias[:, i:i + 1], ins["L0_xattn_" + n].rearrange("(p o) -> p o", o=1))\
                                .then_inc(w_in, 16)
                        m = ins["mask_Bx1x1xS2_bf1"].rearrange("b i j s -> (i j) b s").broadcast_to([P, B, SK])
                        sp.dma_start(mask8[:, :, :], m).then_inc(w_in, 16)
                    else:
                        sp.dma_start(wq[:, :], ins["L1_xattn_W_q"]).then_inc(w_in, 16)
                        for a in range(2):
                            sp.dma_start(wk2[:, a, :], ins["L1_xattn_W_k"]).then_inc(w_in, 16)
                            sp.dma_start(wv2[:, a, :], ins["L1_xattn_W_v"]).then_inc(w_in, 16)
                        sp.dma_start(wo[:, :, :], ins["L1_xattn_W_o"].rearrange("(c p) o -> p c o", p=P))\
                            .then_inc(w_in, 16)

                @block.tensor
                def _(pe):
                    pe.wait_ge(w_in, 16 * (9 if first else 6))
                    if first:
                        for i, t in enumerate((wk, wv, wo)):
                            last = nc.tensor.transpose(psum[0][:, i * P:(i + 1) * P], t[:, :], ident)
                        last.then_inc(wt_full, 1)
                    else:
                        for g in range(2):
                            for i in range(4):
                                cc = 4 * g + i
                                last = nc.tensor.transpose(psum[g][:, i * P:(i + 1) * P],
                                                           wq[:, cc * P:(cc + 1) * P], ident)
                            last.then_inc(wt_full, 1)
                    pe.wait_ge(wt_done, 1)
                    lk = wkT[:, :] if first else wk2[:, :, :].rearrange("p a d -> p (a d)")
                    lv = wvT[:, :] if first else wv2[:, :, :].rearrange("p a d -> p (a d)")
                    for i, lhs in enumerate((lk, lv)):
                        nc.tensor.matmul(psum[2 + i][:, 0:B * SK], lhs, ctxT[:, :, :].rearrange("p b s -> p (b s)"),
                                         start=True, stop=True).then_inc(kv_full, 1)

                @block.scalar
                def _(act):
                    if first:
                        act.wait_ge(wt_full, 1)
                        nc.scalar.activation(wkT[:, :], psum[0][:, 0:P], ACT.Copy)
                        nc.scalar.activation(wvT[:, :], psum[0][:, P:2 * P], ACT.Copy)
                        nc.scalar.activation(woT[:, :], psum[0][:, 2 * P:3 * P], ACT.Copy).then_inc(wt_done, 1)
                    else:
                        for g in range(2):
                            act.wait_ge(wt_full, g + 1)
                            last = nc.scalar.activation(wqT[:, 4 * g:4 * g + 4, :].rearrange("p c i -> p (c i)"),
                                                        psum[g][:, :], ACT.Copy)
                        last.then_inc(wt_done, 1)
                    for i, t in enumerate((kT, vT)):
                        act.wait_ge(kv_full, i + 1)
                        src = psum[2 + i][:, 0:B * SK].rearrange("p (b s) -> p b s", s=SK)
                        if first:
                            nc.scalar.activation(t[:, :, :], src, ACT.Identity, bias=bias[:, 1 + i:2 + i])
                        else:
                            nc.scalar.activation(t[:, :, :], src, ACT.Copy)

                @block.vector
                def _(dve):
                    if first:
                        dve.wait_ge(w_in, 16 * 9)
                        nc.vector.tensor_scalar(maskf[:, :, :], mask8[:, :, :], -NEG, NEG, ALU.mult, ALU.add)
                        nc.vector.tensor_scalar(bq_rep[:, :], ones[:, :], bias[:, 0:1], None, ALU.mult)
                        dve.wait_ge(wt_done, 1)
                        nc.vector.tensor_tensor(wo_heads[:, :, :], woT[:, :].unsqueeze(1).broadcast_to([P, H, P]),
                                                table("heads8").unsqueeze(2).broadcast_to([P, H, P]), ALU.mult)

                c1.close()
                block = c.enter_context(nc.Block())

                def stage(u, j, back):
                    on = not (isinstance(u, int) and u == 0 and j < back) and \
                        not (isinstance(u, int) and u == B and j >= back)
                    b, t = (u, j - back) if j >= back else (u - 1, j - back + NT)
                    return on, b, t, u * NT + j - back

                def more(u):
                    return not (isinstance(u, int) and u >= B - 1)

                def prepared(eng, u, k):
                    for f in prep.free:
                        eng.wait_ge(f, u * (prep.steady // 2) + (NG + k) // 2)

                def run(eng, body):
                    body(0, NT, True)
                    with eng.Fori(1, B - 1) as u:
                        body(u, NT, True)
                    body(B - 1, NT, False)
                    body(B, 2, False)

                @block.tensor
                def _(pe):
                    prep_c, pt_c = prep.cursor(), pt.cursor()

                    def fill(g):
                        bank, q, full, free = prep_c.next()
                        wait(pe, free, q)
                        g(bank).then_inc(full, 1)

                    def product(bank, lhs, rhs):
                        return nc.tensor.matmul(bank[0:lhs.shape[-1], 0:rhs.shape[-1]], lhs, rhs, start=True, stop=True)

                    def make_g(g):
                        if g >= len(GJ):
                            return
                        h0, nh = GJ[g]
                        if first:
                            k = kv[:, h0:h0 + nh, :].rearrange("p h s -> p (h s)")
                            fill(lambda t: product(t, wq[:, :], k))
                            fill(lambda t: product(t, bq_rep[:, :], k))
                            return

                        def pairs(bank):
                            for i in range(2):
                                last = nc.tensor.matmul(bank[:, 2 * i * SK:2 * (i + 1) * SK], wqT[:, h0 // 2 + i, :],
                                                        kv[:, :, :].rearrange("p a s -> p (a s)"), start=True, stop=True)
                            return last
                        fill(pairs)

                    def make_u(g):
                        if first:
                            rhs = wo_heads[:, 4 * g:4 * g + 4, :].rearrange("p h o -> p (h o)")
                            fill(lambda t: product(t, vv[:, :], rhs))
                            return

                        def heads(bank):
                            for i in range(4):
                                h = 4 * g + i
                                last = nc.tensor.matmul(bank[0:SK, i * P:(i + 1) * P], vv[:, h % 2, :], wo[:, h // 2, :],
                                                        start=True, stop=True)
                            return last
                        fill(heads)

                    def step(u, j):
                        S_, _, _, n = stage(u, j, 0)
                        O_, _, jo, o = stage(u, j, 2)
                        if S_:
                            if j == 0:
                                prepared(pe, u, 0)
                            pe.wait_ge(xs_in, n + 1)
                            wait(pe, sc_done, 3 * n)
                            for k, (h0, nh) in enumerate(HJ):
                                nc.tensor.matmul(psum[k][:, 0:nh * SK], xs[:, j % 2, :],
                                                 G[:, h0:h0 + nh, :].rearrange("p h s -> p (h s)"),
                                                 start=True, stop=True).then_inc(sc_full, 1)
                        moved = []

                        def turn(g):
                            if not O_:
                                return
                            if g == 0:
                                pe.wait_ge(p_done, o + 1)
                            bank, q, full, free = pt_c.next()
                            wait(pe, free, q)
                            for i in range(4):
                                last = nc.tensor.transpose(bank[0:SK, i * P:(i + 1) * P], ex[:, jo, 4 * g + i, :], ident)
                            last.then_inc(full, 1)
                            moved.append((free, q + 1))

                        def outputs(g):
                            if not O_:
                                return
                            if g == 0:
                                wait(pe, o_done, o)
                            pe.wait_ge(*moved[g])
                            for h in range(4 * g, 4 * g + 4):
                                last = nc.tensor.matmul(psum[7][:, 0:P], U[:, h, :], pT[:, jo % 2, h, :],
                                                        start=(h == 0), stop=(h == H - 1))
                            if g == 3:
                                last.then_inc(o_full, 1)

                        if S_ and j == 1:
                            pe.wait_ge(vv_in, u + 1)
                        if S_ and j == 2:
                            prepared(pe, u, 4)
                        if j == 3 and more(u):
                            pe.wait_ge(kv_in, u + 2)
                        turn(0)
                        for g in range(4):
                            if g < 3:
                                turn(g + 1)
                            outputs(g)
                            if j == 1 and S_:
                                make_u(g)
                            if j == 3 and more(u):
                                make_g(g)

                    def body(u, steps, check):
                        prep_c.begin(u)
                        pt_c.begin(u)
                        if isinstance(u, int) and u == 0:
                            pe.wait_ge(kv_in, 1)
                            for g in range(4):
                                make_g(g)
                        for j in range(steps):
                            step(u, j)
                        if check:
                            prep_c.end()
                            pt_c.end()

                    run(pe, body)

                @block.scalar
                def _(act):
                    prep_c, pt_c = prep.cursor(), pt.cursor()

                    def take(dst, width, rows=P, scale=1.0):
                        bank, q, full, free = prep_c.next()
                        act.wait_ge(full, q + 1)
                        nc.scalar.activation(dst, bank[0:rows, 0:width], ACT.Copy, scale=scale).then_inc(free, 1)

                    def take_g(g, read):
                        if g >= len(GJ):
                            return
                        h0, nh = GJ[g]
                        take(G[:, h0:h0 + nh, :].rearrange("p h s -> p (h s)"), nh * SK)
                        if first:
                            wait(act, sc_done, read)
                            take(mask_b[:, h0:h0 + nh, :].rearrange("p h s -> p (h s)"), nh * SK, scale=scale)

                    def take_u(g):
                        take(U[:, 4 * g:4 * g + 4, :].rearrange("p h o -> p (h o)"), 4 * P, rows=SK)

                    def step(u, j):
                        S_, _, _, n = stage(u, j, 0)
                        O_, _, jo, o = stage(u, j, 2)

                        def copy(g):
                            if not O_:
                                return
                            if g == 0:
                                wait(act, o_done, o - 1)
                            bank, q, full, free = pt_c.next()
                            act.wait_ge(full, q + 1)
                            nc.scalar.activation(pT[:, jo % 2, 4 * g:4 * g + 4, :].rearrange("p h o -> p (h o)"),
                                                 bank[0:SK, :], ACT.Copy).then_inc(free, 1)

                        copy(0)
                        for g in range(4):
                            if g < 3:
                                copy(g + 1)
                            if j == 1 and S_:
                                take_u(g)
                            if j == 3 and more(u):
                                take_g(g, 3 * n + 3)
                        if S_:
                            act.wait_ge(sub_done, n + 1)
                            e = ex[:, j, :, :].rearrange("p h s -> p (h s)")
                            nc.scalar.activation(e, e, ACT.Exp).then_inc(ex_done, 1)

                    def body(u, steps, check):
                        prep_c.begin(u)
                        pt_c.begin(u)
                        if isinstance(u, int) and u == 0:
                            for g in range(4):
                                take_g(g, 0)
                        for j in range(steps):
                            step(u, j)
                        if check:
                            prep_c.end()
                            pt_c.end()

                    run(act, body)

                @block.vector
                def _(dve):
                    chain = Chain(dve, self_v, NT - 1 + first, NT + first)

                    def masked(dst, src, b):
                        heads = table("heads8" if first else "halves")
                        nh = dst.shape[1]
                        return nc.vector.tensor_tensor(dst[:, :, :], src[:, b, :].unsqueeze(1).broadcast_to([P, nh, SK]),
                                                       heads.unsqueeze(2).broadcast_to([P, nh, SK]), ALU.mult)

                    def step(u, j):
                        S_, b, _, n = stage(u, j, 0)
                        M_, _, jm, m = stage(u, j, 1)
                        O_, bo, jo, o = stage(u, j, 2)
                        if M_:
                            dve.wait_ge(ex_done, m + 1)
                            wait(dve, p_done, m - 1)
                            chain.link(nc.vector.tensor_reduce(den[:, :], ex[:, jm, :, :], X, ALU.add))
                            nc.vector.reciprocal(rden[:, jm % 2, :], den[:, :]).then_inc(rd_done, 1)
                        if S_ and j == 0:
                            wait(dve, o_done, u * NT - 2)
                            if first:
                                nc.vector.tensor_copy(vv[:, :], vT[:, b, :]).then_inc(vv_in, 1)
                                prepared(dve, u, 0)
                                chain.link(nc.vector.tensor_tensor(
                                    mask_b[:, :, :], mask_b[:, :, :],
                                    maskf[:, b, :].unsqueeze(1).broadcast_to([P, H, SK]), ALU.add))
                            else:
                                masked(vv, vT, b).then_inc(vv_in, 1)
                        if S_:
                            wait(dve, sub_done, n - 1)
                            for k, (h0, nh) in enumerate(HJ):
                                dve.wait_ge(sc_full, 3 * n + k + 1)
                                if first:
                                    add = mask_b[:, h0:h0 + nh, :]
                                else:
                                    add = table("causal")[:, j * SK:(j + 1) * SK].unsqueeze(1).broadcast_to([P, nh, SK])
                                nc.vector.scalar_tensor_tensor(
                                    out=sm[:, j % 2, h0:h0 + nh, :],
                                    in0=psum[k][:, 0:nh * SK].rearrange("p (h s) -> p h s", s=SK),
                                    scalar=scale, in1=add, op0=ALU.mult, op1=ALU.add).then_inc(sc_done, 1)
                            dve.wait_ge(sc_done, 3 * n + 3)
                            nc.vector.tensor_reduce(mx[:, j % 2, :], sm[:, j % 2, :, :], X, ALU.max).then_inc(mx_done, 1)
                        if j == 2 and more(u):
                            masked(kv, kT, u + 1).then_inc(kv_in, 1)
                        if O_:
                            dve.wait_ge(o_full, o + 1)
                            xt = xT[:, bo, jo * P:(jo + 1) * P]
                            if first:
                                nc.vector.scalar_tensor_tensor(out=xt, in0=psum[7][:, 0:P], scalar=bias[:, 3:4], in1=xt,
                                                               op0=ALU.add, op1=ALU.add).then_inc(o_done, 1)
                            else:
                                nc.vector.tensor_tensor(xt, psum[7][:, 0:P], xt, ALU.add).then_inc(o_done, 1)

                    def body(u, steps, check):
                        chain.begin(u)
                        if isinstance(u, int) and u == 0:
                            masked(kv, kT, 0).then_inc(kv_in, 1)
                        for j in range(steps):
                            step(u, j)
                        if check:
                            chain.end()

                    run(dve, body)

                @block.gpsimd
                def _(pool):
                    def inputs(b, j, n):
                        wait(pool, sc_done, 3 * n - 3)
                        nc.gpsimd.tensor_copy(xs[:, j % 2, :], yT[:, b, 1 + j * P:1 + (j + 1) * P]).then_inc(xs_in, 1)

                    def step(u, j):
                        S_, _, _, n = stage(u, j, 0)
                        M_, _, jm, m = stage(u, j, 1)
                        if S_ and j < NT - 1:
                            inputs(u, j + 1, n + 1)
                        elif S_ and more(u):
                            inputs(u + 1, 0, n + 1)
                        if M_:
                            pool.wait_ge(rd_done, m + 1)
                            nc.gpsimd.tensor_tensor(ex[:, jm, :, :], ex[:, jm, :, :],
                                                    rden[:, jm % 2, :].unsqueeze(2).broadcast_to([P, H, SK]),
                                                    ALU.mult).then_inc(p_done, 1)
                        if S_:
                            pool.wait_ge(mx_done, n + 1)
                            wait(pool, o_done, n - 3)
                            nc.gpsimd.tensor_tensor(ex[:, j, :, :], sm[:, j % 2, :, :],
                                                    mx[:, j % 2, :].unsqueeze(2).broadcast_to([P, H, SK]),
                                                    ALU.subtract).then_inc(sub_done, 1)

                    def body(u, steps, check):
                        if isinstance(u, int) and u == 0:
                            inputs(0, 0, 0)
                        for j in range(steps):
                            step(u, j)

                    run(pool, body)

        if "A" in phases:
            layernorm(x_of, y_of)
            cross("A")
        if "B" in phases:
            layernorm(x_of, y_of)
            local(nc, ctx, locals())
        if "C" in phases:
            layernorm(x_of, y_of)
            cross("C")
        if "D" in phases:
            layernorm(x_of, y_of)
            experts(nc, ctx, locals())

        with ExitStack() as c:
            otok = sb("otok", [P, B * NT, P], c)
            xt_full, out_in, stored = sem("ot_full", c), sem("out_in", c), sem("stored", c)
            block = c.enter_context(nc.Block())

            @block.tensor
            def _(pe):
                for b in range(B):
                    for t in range(NT):
                        last = nc.tensor.transpose(psum[b][:, t * P:(t + 1) * P], xT[:, b, t * P:(t + 1) * P], ident)
                    last.then_inc(xt_full, 1)

            @block.vector
            def _(dve):
                for b in range(B):
                    dve.wait_ge(xt_full, b + 1)
                    nc.vector.tensor_copy(otok[:, b * NT:(b + 1) * NT, :].rearrange("p t d -> p (t d)"), psum[b][:, :])\
                        .then_inc(out_in, 1)

            @block.sync
            def _(sp):
                for b in range(B):
                    sp.wait_ge(out_in, b + 1)
                    sp.dma_start(out[b, :, :].rearrange("(t p) d -> p t d", p=P), otok[:, b * NT:(b + 1) * NT, :])\
                        .then_inc(stored, 16)
                sp.wait_ge(stored, 16 * B)


NAMES = ["x", "ctx_1024", "mask_Bx1x1xS2_bf1", "L0_xattn_w_q", "L0_xattn_b_q", "L0_xattn_w_k", "L0_xattn_b_k",
         "L0_xattn_w_v", "L0_xattn_b_v", "L0_xattn_w_o", "L0_xattn_b_o", "L0_ffn_Wqkv", "L0_ffn_q_scale",
         "L0_ffn_k_scale", "L0_ffn_Wo", "L0_ffn_ln_g", "L0_ffn_ln_b", "L0_ffn_W1", "L0_ffn_b1", "L0_ffn_W2",
         "L0_ffn_b2", "L1_xattn_W_q", "L1_xattn_W_k", "L1_xattn_W_v", "L1_xattn_W_o", "L1_ffn_Wg", "L1_ffn_bg",
         "L1_ffn_W1", "L1_ffn_b1", "L1_ffn_W2", "L1_ffn_b2"]


def kernel(**inputs):
    import concourse.bacc as bacc
    from concourse.bass_utils import run_bass_kernel_spmd

    nc = bacc.Bacc("TRN2", target_bir_lowering=False, num_devices=1)
    arrays, aps = {}, {}
    for name in NAMES:
        a = np.ascontiguousarray(inputs[name])
        if a.dtype == np.bool_:
            a = a.view(np.uint8)
        if name in ("L0_ffn_ln_g", "L0_ffn_ln_b", "L0_ffn_b2"):
            a = np.ascontiguousarray(a.T)
        if name == "L0_ffn_b1":
            a = np.pad(a.reshape(DEPTH, 2, FI), ((0, 0), (0, 0), (0, 3 * P - FI)))
            a = np.ascontiguousarray(a.reshape(DEPTH, 2, 3, P).transpose(3, 0, 1, 2))
        if name == "L1_ffn_b1":
            a = np.ascontiguousarray(a.reshape(E, FF // P, P).transpose(2, 0, 1))
        arrays[name] = a
        aps[name] = nc.dram_tensor(name, a.shape, mybir.dt.from_np(a.dtype), kind="ExternalInput").ap()
    consts, place = constants()
    arrays["shape_tables"] = consts
    tables = nc.dram_tensor("shape_tables", consts.shape, F32, kind="ExternalInput").ap()
    out = nc.dram_tensor("out", (B, S, P), F32, kind="ExternalOutput").ap()
    net(nc, aps, out, tables, place)
    r = run_bass_kernel_spmd(nc, [arrays], core_ids=[0])
    return r.results[0]["out"]
```
